# Optimizing a Trainium2 kernel written in Bass

```python
import numpy as np
import jax
import jax.numpy as jnp

def _softmax(x, axis=-1):
    return jax.nn.softmax(x, axis=axis)

def _gelu(x):
    return jax.nn.gelu(x, approximate=True)

def _silu(x):
    return jax.nn.silu(x)

def _sigmoid(x):
    return jax.nn.sigmoid(x)

def _layernorm(x, axis=-1, eps=1e-05):
    m = jnp.mean(x, axis=axis, keepdims=True)
    v = jnp.var(x, axis=axis, keepdims=True)
    return (x - m) / jnp.sqrt(v + eps)

def _scatter_add(tgt, idx, src, axis=0):
    return tgt.at[idx].add(src)

def _segment_sum(src, seg, n):
    return jax.ops.segment_sum(src, seg, n)
kernel_name = 'mk_conv_seq_d1_conv_nhwc256_r4_7c1208'

def setup_inputs(seed: int=0):
    np.random.seed(seed)
    _w = jnp.asarray

    def _rec_inputs():
        import jax
        import jax.numpy as jnp
        _gk = jax.random.key(seed)
        x = -0.0002091 + 1 * jax.random.normal(jax.random.fold_in(_gk, 1), (32, 56, 56, 64), jnp.float32)
        return x
    x = _rec_inputs()

    def _L0_conv_setup():
        import jax, jax.numpy as jnp
        import numpy as np
        WS = (7, 7)
        SS = (3, 3)
        NUM_HEADS = 8
        NEG = -1000000000.0

        def _rel_index(ws):
            Wh, Ww = ws
            ch, cw = np.meshgrid(np.arange(Wh), np.arange(Ww), indexing='ij')
            coords = np.stack([ch, cw]).reshape(2, -1)
            rel = coords[:, :, None] - coords[:, None, :]
            rel = rel.transpose(1, 2, 0).astype(np.int64)
            rel[..., 0] += Wh - 1
            rel[..., 1] += Ww - 1
            rel[..., 0] *= 2 * Ww - 1
            return rel.sum(-1)

        def _swin_mask(H, W, ws, ss):
            img = np.zeros((H, W))
            hs = (slice(0, -ws[0]), slice(-ws[0], -ss[0]), slice(-ss[0], None)) if 0 < ss[0] < ws[0] else (slice(None),)
            wsl = (slice(0, -ws[1]), slice(-ws[1], -ss[1]), slice(-ss[1], None)) if 0 < ss[1] < ws[1] else (slice(None),)
            cnt = 0
            for h in hs:
                for w in wsl:
                    img[h, w] = cnt
                    cnt += 1
            m = img.reshape(H // ws[0], ws[0], W // ws[1], ws[1]).transpose(0, 2, 1, 3).reshape(-1, ws[0] * ws[1])
            diff = m[:, None, :] - m[:, :, None]
            return np.where(diff != 0, NEG, 0.0).astype(np.float32)

        def _coords_table(ws, h_times, ws_scalar, ws_scalar2, pow_para):
            Wh, Ww = ws
            ch = jnp.arange(-(Wh - 1), Wh, dtype=jnp.float32) / max(Wh - 1, 1)
            cw = jnp.arange(-(Ww - 1), Ww, dtype=jnp.float32) / max(Ww - 1, 1)
            tab = jnp.stack(jnp.meshgrid(ch, cw, indexing='ij'), axis=-1)
            tab = tab * h_times
            tab = jnp.sign(tab) * jnp.power(jnp.abs(tab) * ws_scalar + 1e-06, pow_para) / ws_scalar2
            return tab.reshape(-1, 2)

        def _ln(x, w, b):
            mu = x.mean(-1, keepdims=True)
            var = x.var(-1, keepdims=True)
            return (x - mu) / jnp.sqrt(var + 1e-05) * w + b
        key = jax.random.key(seed)
        ks = jax.random.split(key, 8)
        B, H, W, C = (32, 56, 56, 64)
        hid = 4 * C
        s = 0.02
        return {'x': jax.random.normal(ks[0], (B, H, W, C), jnp.float32), 'norm1_w': jnp.ones((C,), jnp.float32), 'norm1_b': jnp.zeros((C,), jnp.float32), 'qkv_w': jax.random.normal(ks[1], (3 * C, C), jnp.float32) * s, 'proj_w': jax.random.normal(ks[2], (C, C), jnp.float32) * s, 'proj_b': jnp.zeros((C,), jnp.float32), 'cpb_w1': jax.random.normal(ks[3], (128, 2), jnp.float32) * s, 'cpb_b1': jnp.zeros((128,), jnp.float32), 'cpb_w2': jax.random.normal(ks[4], (NUM_HEADS, 128), jnp.float32) * s, 'h_times': jnp.asarray(2.0, jnp.float32), 'pow_para': jnp.asarray(0.0, jnp.float32), 'ws_scalar': jnp.asarray(1.0, jnp.float32), 'ws_scalar2': jnp.asarray(2.0, jnp.float32), 'norm2_w': jnp.ones((C,), jnp.float32), 'norm2_b': jnp.zeros((C,), jnp.float32), 'fc1_w': jax.random.normal(ks[5], (hid, C), jnp.float32) * s, 'fc1_b': jnp.zeros((hid,), jnp.float32), 'fc2_w': jax.random.normal(ks[6], (C, hid), jnp.float32) * s, 'fc2_b': jnp.zeros((C,), jnp.float32)}
    _L0_conv_all = _L0_conv_setup()
    _L0_conv_in = {k: v for k, v in _L0_conv_all.items() if k in ('norm1_w', 'norm1_b', 'qkv_w', 'proj_w', 'proj_b', 'cpb_w1', 'cpb_b1', 'cpb_w2', 'h_times', 'pow_para', 'ws_scalar', 'ws_scalar2', 'norm2_w', 'norm2_b', 'fc1_w', 'fc1_b', 'fc2_w', 'fc2_b')}
    del _L0_conv_all
    return {'x': x, 'L0_conv_norm1_w': _L0_conv_in['norm1_w'], 'L0_conv_norm1_b': _L0_conv_in['norm1_b'], 'L0_conv_qkv_w': _L0_conv_in['qkv_w'], 'L0_conv_proj_w': _L0_conv_in['proj_w'], 'L0_conv_proj_b': _L0_conv_in['proj_b'], 'L0_conv_cpb_w1': _L0_conv_in['cpb_w1'], 'L0_conv_cpb_b1': _L0_conv_in['cpb_b1'], 'L0_conv_cpb_w2': _L0_conv_in['cpb_w2'], 'L0_conv_h_times': _L0_conv_in['h_times'], 'L0_conv_pow_para': _L0_conv_in['pow_para'], 'L0_conv_ws_scalar': _L0_conv_in['ws_scalar'], 'L0_conv_ws_scalar2': _L0_conv_in['ws_scalar2'], 'L0_conv_norm2_w': _L0_conv_in['norm2_w'], 'L0_conv_norm2_b': _L0_conv_in['norm2_b'], 'L0_conv_fc1_w': _L0_conv_in['fc1_w'], 'L0_conv_fc1_b': _L0_conv_in['fc1_b'], 'L0_conv_fc2_w': _L0_conv_in['fc2_w'], 'L0_conv_fc2_b': _L0_conv_in['fc2_b']}

def reference(x, L0_conv_norm1_w, L0_conv_norm1_b, L0_conv_qkv_w, L0_conv_proj_w, L0_conv_proj_b, L0_conv_cpb_w1, L0_conv_cpb_b1, L0_conv_cpb_w2, L0_conv_h_times, L0_conv_pow_para, L0_conv_ws_scalar, L0_conv_ws_scalar2, L0_conv_norm2_w, L0_conv_norm2_b, L0_conv_fc1_w, L0_conv_fc1_b, L0_conv_fc2_w, L0_conv_fc2_b):
    import jax
    import jax.numpy as jnp

    def _L0_conv_ref(x, norm1_w, norm1_b, qkv_w, proj_w, proj_b, cpb_w1, cpb_b1, cpb_w2, h_times, pow_para, ws_scalar, ws_scalar2, norm2_w, norm2_b, fc1_w, fc1_b, fc2_w, fc2_b):
        import jax, jax.numpy as jnp
        import numpy as np
        WS = (7, 7)
        SS = (3, 3)
        NUM_HEADS = 8
        NEG = -1000000000.0

        def _rel_index(ws):
            Wh, Ww = ws
            ch, cw = np.meshgrid(np.arange(Wh), np.arange(Ww), indexing='ij')
            coords = np.stack([ch, cw]).reshape(2, -1)
            rel = coords[:, :, None] - coords[:, None, :]
            rel = rel.transpose(1, 2, 0).astype(np.int64)
            rel[..., 0] += Wh - 1
            rel[..., 1] += Ww - 1
            rel[..., 0] *= 2 * Ww - 1
            return rel.sum(-1)

        def _swin_mask(H, W, ws, ss):
            img = np.zeros((H, W))
            hs = (slice(0, -ws[0]), slice(-ws[0], -ss[0]), slice(-ss[0], None)) if 0 < ss[0] < ws[0] else (slice(None),)
            wsl = (slice(0, -ws[1]), slice(-ws[1], -ss[1]), slice(-ss[1], None)) if 0 < ss[1] < ws[1] else (slice(None),)
            cnt = 0
            for h in hs:
                for w in wsl:
                    img[h, w] = cnt
                    cnt += 1
            m = img.reshape(H // ws[0], ws[0], W // ws[1], ws[1]).transpose(0, 2, 1, 3).reshape(-1, ws[0] * ws[1])
            diff = m[:, None, :] - m[:, :, None]
            return np.where(diff != 0, NEG, 0.0).astype(np.float32)

        def _coords_table(ws, h_times, ws_scalar, ws_scalar2, pow_para):
            Wh, Ww = ws
            ch = jnp.arange(-(Wh - 1), Wh, dtype=jnp.float32) / max(Wh - 1, 1)
            cw = jnp.arange(-(Ww - 1), Ww, dtype=jnp.float32) / max(Ww - 1, 1)
            tab = jnp.stack(jnp.meshgrid(ch, cw, indexing='ij'), axis=-1)
            tab = tab * h_times
            tab = jnp.sign(tab) * jnp.power(jnp.abs(tab) * ws_scalar + 1e-06, pow_para) / ws_scalar2
            return tab.reshape(-1, 2)

        def _ln(x, w, b):
            mu = x.mean(-1, keepdims=True)
            var = x.var(-1, keepdims=True)
            return (x - mu) / jnp.sqrt(var + 1e-05) * w + b
        B, H, W, C = x.shape
        h = NUM_HEADS
        d = C // h
        scale = d ** (-0.5)
        nWh, nWw = (H // WS[0], W // WS[1])
        nW = nWh * nWw
        N = WS[0] * WS[1]
        shortcut = x
        y = _ln(x, norm1_w, norm1_b)
        y = jnp.roll(y, (-SS[0], -SS[1]), axis=(1, 2))
        win = y.reshape(B, nWh, WS[0], nWw, WS[1], C).transpose(0, 1, 3, 2, 4, 5).reshape(B * nW, N, C)
        qkv = (win @ qkv_w.T).reshape(B * nW, N, 3, h, d).transpose(2, 0, 3, 1, 4)
        q, k, v = (qkv[0], qkv[1], qkv[2])
        attn = jnp.einsum('bhnd,bhmd->bhnm', q, k) * scale
        tab = _coords_table(WS, jax.nn.softplus(h_times), jax.nn.softplus(ws_scalar), jax.nn.softplus(ws_scalar2), jax.nn.sigmoid(pow_para))
        tb = jax.nn.relu(tab @ cpb_w1.T + cpb_b1) @ cpb_w2.T
        idx = jnp.asarray(_rel_index(WS))
        bias = tb[idx.reshape(-1)].reshape(N, N, h).transpose(2, 0, 1)
        attn = attn + bias[None]
        mask = jnp.asarray(_swin_mask(H, W, WS, SS))
        attn = attn.reshape(B, nW, h, N, N) + mask[None, :, None]
        attn = jax.nn.softmax(attn.reshape(B * nW, h, N, N), axis=-1)
        out = jnp.einsum('bhnm,bhmd->bhnd', attn, v).transpose(0, 2, 1, 3).reshape(B * nW, N, C)
        out = out @ proj_w.T + proj_b
        out = out.reshape(B, nWh, nWw, WS[0], WS[1], C).transpose(0, 1, 3, 2, 4, 5).reshape(B, H, W, C)
        out = jnp.roll(out, (SS[0], SS[1]), axis=(1, 2))
        x = shortcut + out
        z = _ln(x, norm2_w, norm2_b)
        z = jax.nn.gelu(z @ fc1_w.T + fc1_b, approximate=False) @ fc2_w.T + fc2_b
        return x + z

    def _gn(v, G=32, eps=1e-05):
        B_, H_, W_, C_ = v.shape
        g = v.reshape(B_, H_, W_, G, C_ // G)
        m = jnp.mean(g, axis=(1, 2, 4), keepdims=True)
        s = jnp.var(g, axis=(1, 2, 4), keepdims=True)
        return ((g - m) / jnp.sqrt(s + eps)).reshape(v.shape)

    def _ln_c(v, eps=1e-06):
        m = jnp.mean(v, axis=-1, keepdims=True)
        s = jnp.var(v, axis=-1, keepdims=True)
        return (v - m) / jnp.sqrt(s + eps)

    def _ln_t(v, eps=1e-05):
        m = jnp.mean(v, axis=-1, keepdims=True)
        s = jnp.var(v, axis=-1, keepdims=True)
        return (v - m) / jnp.sqrt(s + eps)

    def _to_tokens(v):
        B_, H_, W_, C_ = v.shape
        return v.reshape(B_, H_ * W_, C_)

    def _from_tokens(t, like):
        return t.reshape(like.shape)
    x = _L0_conv_ref(x, L0_conv_norm1_w, L0_conv_norm1_b, L0_conv_qkv_w, L0_conv_proj_w, L0_conv_proj_b, L0_conv_cpb_w1, L0_conv_cpb_b1, L0_conv_cpb_w2, L0_conv_h_times, L0_conv_pow_para, L0_conv_ws_scalar, L0_conv_ws_scalar2, L0_conv_norm2_w, L0_conv_norm2_b, L0_conv_fc1_w, L0_conv_fc1_b, L0_conv_fc2_w, L0_conv_fc2_b)
    return x

_drawn_inputs = setup_inputs


def setup_inputs(seed=0):
    import zlib

    import numpy as np

    out = dict(_drawn_inputs(seed))
    spreads = {'L0_conv_norm1_w': (1.0, 0.6),
     'L0_conv_norm1_b': (0.0, 0.8),
     'L0_conv_proj_b': (0.0, 0.1),
     'L0_conv_cpb_b1': (0.0, 2.0),
     'L0_conv_norm2_w': (1.0, 0.6),
     'L0_conv_norm2_b': (0.0, 2.0),
     'L0_conv_fc1_b': (0.0, 0.444),
     'L0_conv_fc2_b': (0.0, 0.1)}
    factors = {'L0_conv_qkv_w': 8.0,
     'L0_conv_proj_w': 8.0,
     'L0_conv_cpb_w1': 8.0,
     'L0_conv_cpb_w2': 24.767,
     'L0_conv_fc1_w': 3.079}
    for name, (base, spread) in spreads.items():
        noise = np.random.default_rng([zlib.crc32(name.encode()), seed]).standard_normal(out[name].shape)
        drawn = base * np.exp(spread * noise) if base else spread * noise
        out[name] = jnp.asarray(drawn.astype(out[name].dtype))
    for name, factor in factors.items():
        out[name] = (out[name] * factor).astype(out[name].dtype)
    return out
```

```python
from contextlib import ExitStack

import numpy as np

import concourse.bass as bass
from concourse import mybir

F32 = mybir.dt.float32
BF16 = mybir.dt.bfloat16
F16 = mybir.dt.float16
ACT = mybir.ActivationFunctionType
ALU = mybir.AluOpType
AX_X = mybir.AxisListType.X

WIN = 7
N = WIN * WIN
SHIFT = 3
HEADS = 8
D = 8
C = HEADS * D
HID = 4 * C
PAIRS = 4
W0 = 64
R = W0 + N
T = PAIRS * 2 * N
HK = HEADS * N
QKH = 2 * HEADS
HR = 32
TP = R + 1
TABLE = (2 * WIN - 1) ** 2
TCH = (TABLE + 1) // 2
VC = 2 * D + 2
EPS = 1e-5
U = 8
XRING = 4


def swin_block(nc, x, norm1_w, norm1_b, qkv_wT, proj_wT, proj_b, cpb_w1T, cpb_b1, cpb_w2T, h_times,
               pow_para, ws_scalar, ws_scalar2, norm2_w, norm2_b, fc1_wT, fc1_b, fc2_wT, fc2_b,
               c_ident, c_onehot, c_mask, c_grid, c_headsel, c_densel, out):
    NB = x.shape[0]
    NSB = NB // 2
    ctx = ExitStack()
    with ctx:
        def sb(name, shape, dt=F32):
            return ctx.enter_context(nc.sbuf_tensor(name, shape, dt))

        def ps(name):
            return ctx.enter_context(nc.psum_tensor(name, [128, 512], F32))

        def sem(name):
            return ctx.enter_context(nc.semaphore(name))

        ident = sb("ident", [128, 128])
        identb = sb("identb", [128, 128], BF16)
        identh = sb("identh", [128, 128], F16)
        onehot = sb("onehot", [TCH, 2, N, R])
        maskc = sb("maskc", [R, 4, N])
        grid = sb("grid", [2, TABLE])
        headsel_f = sb("headsel_f", [HEADS, HK])
        headsel = sb("headsel", [HEADS, HK], BF16)
        densel = sb("densel", [128, 128])
        n1w, n1b = sb("n1w", [R, C]), sb("n1b", [R, C])
        n2w, n2b = sb("n2w", [R, C]), sb("n2b", [R, C])
        projb, fc2b = sb("projb", [R, C]), sb("fc2b", [R, C])
        wqkv = sb("wqkv", [2 * C, 3 * C])
        wproj = sb("wproj", [128, C])
        w1 = sb("w1", [2 * C, HID])
        w2 = sb("w2", [128, 2, C])
        b1 = sb("b1", [128, 2])
        cpbw1 = sb("cpbw1", [2, 128])
        cpbb1 = sb("cpbb1", [128, 1])
        cpbw2 = sb("cpbw2", [128, HEADS])
        scal = sb("scal", [2, 4])
        st = sb("st", [2, 12, 4])
        tab = sb("tab", [2, 6, TABLE])
        hidden = sb("hidden", [128, 2 * TCH])
        tbs = sb("tbs", [TCH, 2, HEADS])
        mhalf = sb("mhalf", [R, PAIRS])
        bias_t = sb("bias_t", [R, 2, HK])
        biasp = sb("biasp", [R, 4 * 3, HK], BF16)

        xin = [sb(f"xin{b}", [R, PAIRS, C]) for b in range(2)]
        xres = sb("xres", [R, XRING * 2, PAIRS * C])
        stats = [sb(f"stats{b}", [R, PAIRS, 6]) for b in range(2)]
        mv = [sb(f"mv{b}", [R, PAIRS, 2]) for b in range(2)]
        veps = [sb(f"veps{b}", [R, PAIRS]) for b in range(2)]
        rstd = [sb(f"rstd{b}", [R, PAIRS]) for b in range(2)]
        y0 = [sb(f"y0{b}", [R, PAIRS, C]) for b in range(2)]
        y1 = [sb(f"y1{b}", [R, PAIRS, C]) for b in range(2)]
        y2 = [sb(f"y2{b}", [R, PAIRS, C]) for b in range(2)]
        yT = [sb(f"yT{b}", [2 * C, 2, 128]) for b in range(2)]
        qkp = [sb(f"qkp{b}", [R, PAIRS, QKH, HR], F16) for b in range(2)]
        vs = [sb(f"vs{b}", [R, PAIRS, C]) for b in range(2)]
        qx = [sb(f"qx{b}", [128, 2 * PAIRS, TP], F16) for b in range(2)]
        kx = [sb(f"kx{b}", [128, 4, 2 * PAIRS, TP], F16) for b in range(2)]
        vx = [sb(f"vx{b}", [R, 2 * PAIRS, 4, VC]) for b in range(2)]
        nm = [sb(f"nm{n}", [R, HEADS], BF16) for n in range(2)]
        nmT = [sb(f"nmT{n}", [HEADS, 114], BF16) for n in range(2)]
        probs = [sb(f"probs{n}", [R, HEADS, W0]) for n in range(2)]
        pT = [sb(f"pT{n}", [R, 4, R]) for n in range(2)]
        o_sb = [sb(f"o_sb{b}", [128, T]) for b in range(2)]
        rec = [sb(f"rec{b}", [128, T]) for b in range(2)]
        on = [sb(f"on{b}", [128, 2 * PAIRS, W0]) for b in range(2)]
        x1 = [sb(f"x1{b}", [R, PAIRS, C]) for b in range(2)]
        x1b = [sb(f"x1b{b}", [R, PAIRS, C]) for b in range(2)]
        stats2 = [sb(f"stats2{b}", [R, PAIRS, 6]) for b in range(2)]
        mv2 = [sb(f"mv2{b}", [R, PAIRS, 2]) for b in range(2)]
        veps2 = [sb(f"veps2{b}", [R, PAIRS]) for b in range(2)]
        rstd2 = [sb(f"rstd2{b}", [R, PAIRS]) for b in range(2)]
        z0 = [sb(f"z0{b}", [R, PAIRS, C]) for b in range(2)]
        z1 = [sb(f"z1{b}", [R, PAIRS, C]) for b in range(2)]
        z2 = [sb(f"z2{b}", [R, PAIRS, C]) for b in range(2)]
        zT = [sb(f"zT{b}", [2 * C, T // 2]) for b in range(2)]
        gl = [sb(f"gl{b}", [128, 2, T]) for b in range(2)]
        mT = [sb(f"mT{b}", [2 * C, PAIRS, W0]) for b in range(2)]
        res = [sb(f"res{b}", [R, PAIRS, C]) for b in range(2)]

        S = [ps(f"S{n}") for n in range(3)]
        PT = [ps(f"PT{n}") for n in range(2)]
        O = ps("O")
        MI = [ps("MA"), ps("MB")]
        NMT_COL = 4 * R

        c_in = sem("c_in")
        c_zero = sem("c_zero")
        c_chain = sem("c_chain")
        c_ready = sem("c_ready")
        c_act = sem("c_act")
        c_pool = sem("c_pool")
        c_pe = sem("c_pe")
        s_x = [sem(f"s_x{b}") for b in range(2)]
        s_st = [sem(f"s_st{b}") for b in range(2)]
        s_rs = [sem(f"s_rs{b}") for b in range(2)]
        s_y0 = [sem(f"s_y0{b}") for b in range(2)]
        s_y1 = [sem(f"s_y1{b}") for b in range(2)]
        s_y2 = [sem(f"s_y2{b}") for b in range(2)]
        s_xres = [sem(f"s_xres{b}") for b in range(2)]
        s_yTp = [sem(f"s_yTp{b}") for b in range(2)]
        s_yT = [sem(f"s_yT{b}") for b in range(2)]
        s_qkv = [sem(f"s_qkv{b}") for b in range(2)]
        s_hi = [sem(f"s_hi{b}") for b in range(2)]
        s_vs = [sem(f"s_vs{b}") for b in range(2)]
        s_lo = [sem(f"s_lo{b}") for b in range(2)]
        s_dup = [sem(f"s_dup{b}") for b in range(2)]
        s_qTp = [sem(f"s_qTp{b}") for b in range(2)]
        s_kTp = [sem(f"s_kTp{b}") for b in range(2)]
        s_qx = [sem(f"s_qx{b}") for b in range(2)]
        s_kx = [sem(f"s_kx{b}") for b in range(2)]
        s_vx = [sem(f"s_vx{b}") for b in range(2)]
        s_sc = sem("s_sc")
        s_nm = sem("s_nm")
        s_nmp = sem("s_nmp")
        s_nmT = sem("s_nmT")
        s_sh = sem("s_sh")
        s_e = sem("s_e")
        s_pTp = sem("s_pTp")
        s_pT = sem("s_pT")
        s_pv = sem("s_pv")
        s_o = [sem(f"s_o{b}") for b in range(2)]
        s_den = [sem(f"s_den{b}") for b in range(2)]
        s_rec = [sem(f"s_rec{b}") for b in range(2)]
        s_on = [sem(f"s_on{b}") for b in range(2)]
        s_pj = [sem(f"s_pj{b}") for b in range(2)]
        s_x1 = [sem(f"s_x1{b}") for b in range(2)]
        s_x1b = [sem(f"s_x1b{b}") for b in range(2)]
        s_st2 = [sem(f"s_st2{b}") for b in range(2)]
        s_rs2 = [sem(f"s_rs2{b}") for b in range(2)]
        s_z0 = [sem(f"s_z0{b}") for b in range(2)]
        s_z1 = [sem(f"s_z1{b}") for b in range(2)]
        s_z2 = [sem(f"s_z2{b}") for b in range(2)]
        s_zTp = [sem(f"s_zTp{b}") for b in range(2)]
        s_zT = [sem(f"s_zT{b}") for b in range(2)]
        s_f = [sem(f"s_f{b}") for b in range(2)]
        s_g = [sem(f"s_g{b}") for b in range(2)]
        s_m = [sem(f"s_m{b}") for b in range(2)]
        s_mT = [sem(f"s_mT{b}") for b in range(2)]
        s_mo = [sem(f"s_mo{b}") for b in range(2)]
        s_res = [sem(f"s_res{b}") for b in range(2)]
        s_out = [sem(f"s_out{b}") for b in range(2)]

        N_IN = 30
        ZEROED = 14
        C_ABS, C_POW, C_TAB, C_HID, C_TBS = 3, 13, 18, 19, 22

        def on_chip(u):
            return not isinstance(u, int) or 0 <= u < NSB

        def later(u, k=1):
            return not isinstance(u, int) or u >= k

        def rounds(eng, body):
            for i in range(-1, 2):
                body(i)
            with eng.Fori(2, NSB - 2) as i:
                body(i)
            for i in range(NSB - 2, NSB + 2):
                body(i)

        def at_unit(i, k, back):
            return i + (k - back) // U, (k - back) % U

        def exp_bank(j):
            return S_BANK[j]

        block = ctx.enter_context(nc.Block())

        @block.sync
        def _(sp):
            ins = [(ident[:], c_ident), (onehot[:, 0], c_onehot[0]), (onehot[:, 1], c_onehot[1]),
                   (maskc[:], c_mask), (grid[:], c_grid), (headsel_f[:], c_headsel), (densel[:], c_densel),
                   (n1w[:], norm1_w), (n1b[:], norm1_b), (n2w[:], norm2_w), (n2b[:], norm2_b),
                   (projb[:], proj_b), (fc2b[:], fc2_b), (wqkv[0:C], qkv_wT), (wqkv[C:2 * C], qkv_wT), (w1[0:C], fc1_wT),
                   (w1[C:2 * C], fc1_wT),
                   (w2[:], fc2_wT), (b1[:], fc1_b), (cpbw1[:], cpb_w1T), (cpbb1[:], cpb_b1),
                   (cpbw2[:], cpb_w2T), (scal[:, 0:1], h_times), (scal[:, 1:2], ws_scalar),
                   (scal[:, 2:3], ws_scalar2), (scal[:, 3:4], pow_para)]
            for dst, src in ins:
                sp.dma_start(dst, src).then_inc(c_in, 16)
            sp.wait_ge(c_zero, 1)
            for hp in range(4):
                sp.dma_start(wproj[32 * hp:32 * hp + 16, :], proj_wT[16 * hp:16 * hp + 16, :]).then_inc(c_in, 16)
            sp.wait_ge(c_zero, ZEROED)

            def load(u, b):
                src = [x[2 * u + b, w] for w in range(2)]
                if later(u):
                    sp.wait_ge(s_y0[b], u)
                    sp.wait_ge(s_xres[b], u)
                for w in range(2):
                    sp.dma_start(xin[b][W0 * w:W0 * w + N], src[w]).then_inc(s_x[b], 16)

            def store(u, b):
                sp.wait_ge(s_res[b], u + 1)
                for w in range(2):
                    sp.dma_start(out[2 * u + b, w], res[b][W0 * w:W0 * w + N]).then_inc(s_out[b], 16)

            for b in range(2):
                load(0, b)

            def body(i):
                if on_chip(i - 2):
                    store(i - 2, 0)
                    store(i - 2, 1)
                if on_chip(i + 2):
                    load(i + 2, 0)
                if on_chip(i + 2):
                    load(i + 2, 1)

            rounds(sp, body)
            for b in range(2):
                sp.wait_ge(s_out[b], 32 * NSB)

        @block.gpsimd
        def _(pool):
            nc.gpsimd.memset(wproj[:], 0.0).then_inc(c_zero, 1)
            for b in range(2):
                nc.gpsimd.memset(xin[b][:], 0.0).then_inc(c_zero, 1)
                nc.gpsimd.memset(kx[b][:], 0.0).then_inc(c_zero, 1)
                nc.gpsimd.memset(on[b][:], 0.0).then_inc(c_zero, 1)
                nc.gpsimd.memset(mT[b][:], 0.0).then_inc(c_zero, 1)
                nc.gpsimd.memset(probs[b][:], 0.0).then_inc(c_zero, 1)
                nc.gpsimd.memset(nmT[b][:], 0.0).then_inc(c_zero, 1)
            nc.gpsimd.memset(mhalf[:], -0.5).then_inc(c_zero, 1)
            pool.wait_ge(c_zero, ZEROED)
            pool.wait_ge(c_chain, C_POW)
            nc.gpsimd.tensor_tensor(tab[:, 4, :], tab[:, 3, :], tab[:, 5, :], ALU.pow).then_inc(c_pool, 1)

            def ln_rstd(veps_b, rstd_b, s_veps, s_rs_b, u, s_used):
                pool.wait_ge(s_veps, 9 * u + 9)
                if later(u):
                    pool.wait_ge(s_used, u)
                nc.gpsimd.tensor_tensor(rstd_b[:], veps_b[:], mhalf[:], ALU.pow).then_inc(s_rs_b, 1)

            def affine(a0, a1, a2, w, bvec, s0, s1, s2, s_used, u):
                pool.wait_ge(s0, u + 1)
                if later(u):
                    pool.wait_ge(s2, u)
                nc.gpsimd.tensor_tensor(a1[:], a0[:], w[:].unsqueeze(1).broadcast_to([R, PAIRS, C]), ALU.mult).then_inc(s1, 1)
                pool.wait_ge(s1, u + 1)
                if later(u):
                    pool.wait_ge(s_used, u)
                nc.gpsimd.tensor_tensor(a2[:], a1[:], bvec[:].unsqueeze(1).broadcast_to([R, PAIRS, C]), ALU.add).then_inc(s2, 1)

            def keep_residual(u, b):
                if later(u, XRING):
                    pool.wait_ge(s_x1[b], u - XRING + 1)
                pool.wait_ge(s_x[b], 32 * u + 32)
                nc.gpsimd.tensor_tensor(xres[:, bass.ds((u % XRING) * 2 + b, 1), :].rearrange("r o (p c) -> r (o p) c", p=PAIRS),
                                        xin[b][:], projb[:].unsqueeze(1).broadcast_to([R, PAIRS, C]),
                                        ALU.add).then_inc(s_xres[b], 1)

            def normalise(u, b):
                pool.wait_ge(s_rec[b], u + 1)
                if later(u):
                    pool.wait_ge(s_pj[b], u)
                nc.gpsimd.tensor_tensor(on[b][:, :, 0:N], o_sb[b][:].rearrange("c (w n) -> c w n", n=N),
                                        rec[b][:].rearrange("c (w n) -> c w n", n=N), ALU.mult).then_inc(s_on[b], 1)

            def add_fc2b(u, b):
                pool.wait_ge(s_x1[b], u + 1)
                if later(u):
                    pool.wait_ge(s_res[b], u)
                nc.gpsimd.tensor_tensor(x1b[b][:], x1[b][:], fc2b[:].unsqueeze(1).broadcast_to([R, PAIRS, C]),
                                        ALU.add).then_inc(s_x1b[b], 1)

            def ln1(u, b):
                ln_rstd(veps[b], rstd[b], s_st[b], s_rs[b], u, s_y0[b])
                keep_residual(u, b)
                affine(y0[b], y1[b], y2[b], n1w, n1b, s_y0[b], s_y1[b], s_y2[b], s_yTp[b], u)

            def ln2(u, b):
                ln_rstd(veps2[b], rstd2[b], s_st2[b], s_rs2[b], u, s_z0[b])
                affine(z0[b], z1[b], z2[b], n2w, n2b, s_z0[b], s_z1[b], s_z2[b], s_zTp[b], u)

            def body(i):
                for k in range(U):
                    if k == 0:
                        if on_chip(i - 1):
                            normalise(i - 1, 0)
                        if on_chip(i + 1):
                            ln1(i + 1, 0)
                    if k == 2:
                        if on_chip(i - 1):
                            ln2(i - 1, 0)
                        if on_chip(i + 1):
                            ln1(i + 1, 1)
                    if k == 3:
                        if on_chip(i - 1):
                            normalise(i - 1, 1)
                    if k == 4:
                        if on_chip(i - 1):
                            add_fc2b(i - 1, 0)
                    if k == 5:
                        if on_chip(i - 1):
                            ln2(i - 1, 1)
                            add_fc2b(i - 1, 1)

            rounds(pool, body)

        @block.scalar
        def _(act):
            act.wait_ge(c_chain, C_ABS)
            nc.scalar.activation(st[:, 2, 0:3], st[:, 1, 0:3], ACT.Exp, scale=-1.0).then_inc(c_act, 1)
            nc.scalar.activation(st[:, 3, 0:1], scal[:, 3:4], ACT.Exp, scale=-1.0).then_inc(c_act, 1)
            act.wait_ge(c_act, 2)
            nc.scalar.activation(st[:, 4, 0:3], st[:, 2, 0:3], ACT.Ln, bias=1.0).then_inc(c_act, 1)

            def evac_yT(u, b):
                act.wait_ge(s_yTp[b], u + 1)
                if later(u):
                    act.wait_ge(s_qkv[b], 2 * u)
                nc.scalar.activation(yT[b][:, :, 0:R], MI[Y_BANK[b]][:, 0:2 * R].rearrange("c (p r) -> c p r", p=2),
                                     ACT.Copy).then_inc(s_yT[b], 1)

            def keep_qkv(u, b):
                for h in range(2):
                    bank = MI[1 - h][0:R, 0:2 * 3 * C].rearrange("r (p f) -> r p f", p=2)
                    act.wait_ge(s_qkv[b], 2 * u + h + 1)
                    if later(u):
                        act.wait_ge(s_kTp[b], u)
                        act.wait_ge(s_vx[b], 4 * u)
                    nc.scalar.activation(qkp[b][:, h::2, :, 0:D],
                                         bank[:, :, 0:2 * C].rearrange("r p (h d) -> r p h d", d=D),
                                         ACT.Copy).then_inc(s_hi[b], 1)
                    nc.scalar.activation(vs[b][:, h::2, :], bank[:, :, 2 * C:3 * C], ACT.Copy).then_inc(s_vs[b], 1)

            def exp(u, j):
                n = U * u + j
                act.wait_ge(s_sh, n + 1)
                if later(u) or j >= 2:
                    act.wait_ge(s_pTp, n - 1)
                nc.scalar.activation(probs[j % 2][:, :, 0:N], S[exp_bank(j)][0:R, 0:HK].rearrange("q (h n) -> q h n", n=N),
                                     ACT.Exp).then_inc(s_e, 1)

            def evac_pT(u, j):
                n = U * u + j
                act.wait_ge(s_pTp, n + 1)
                if later(u) or j >= 2:
                    act.wait_ge(s_pv, n - 1)
                nc.scalar.activation(pT[j % 2][:].rearrange("k h r -> k (h r)"), PT[j % 2][0:R, 0:4 * R],
                                     ACT.Copy).then_inc(s_pT, 1)

            def gelu(u, b):
                for c in range(2):
                    act.wait_ge(s_f[b], 4 * u + 3 + c)
                    if later(u):
                        act.wait_ge(s_m[b], u)
                    nc.scalar.activation(gl[b][:, c, :], MI[c][:, 0:T], ACT.Gelu, bias=b1[:, c:c + 1]).then_inc(s_g[b], 1)

            def body(i):
                for k in range(U):
                    u, j = at_unit(i, k, 1)
                    if on_chip(u):
                        exp(u, j)
                    u, j = at_unit(i, k, 2)
                    if on_chip(u):
                        evac_pT(u, j)
                    if k == 1 and on_chip(i + 1):
                        evac_yT(i + 1, 0)
                    if k == 2 and on_chip(i + 1):
                        keep_qkv(i + 1, 0)
                    if k == 4 and on_chip(i + 1):
                        evac_yT(i + 1, 1)
                    if k == 5 and on_chip(i + 1):
                        keep_qkv(i + 1, 1)
                    if k == 7:
                        if on_chip(i - 1):
                            gelu(i - 1, 0)
                            gelu(i - 1, 1)

            rounds(act, body)

        @block.vector
        def _(dve):
            steps = [0]

            def then(ins):
                steps[0] += 1
                ins.then_inc(c_chain, 1)
                dve.wait_ge(c_chain, steps[0])

            V = nc.vector
            dve.wait_ge(c_in, 16 * N_IN)
            then(V.tensor_scalar(st[:, 0, 0:3], scal[:, 0:3], -1.0, None, ALU.mult))
            then(V.tensor_tensor(st[:, 1, 0:3], scal[:, 0:3], st[:, 0, 0:3], ALU.max))
            then(V.tensor_scalar(st[:, 5, 0:3], scal[:, 0:3], 0.0, None, ALU.max))
            dve.wait_ge(c_act, 3)
            then(V.tensor_tensor(st[:, 6, 0:3], st[:, 5, 0:3], st[:, 4, 0:3], ALU.add))
            then(V.tensor_scalar(st[:, 7, 0:1], st[:, 3, 0:1], 1.0, None, ALU.add))
            then(V.reciprocal(st[:, 8, 0:1], st[:, 7, 0:1]))
            then(V.reciprocal(st[:, 9, 0:1], st[:, 6, 2:3]))
            then(V.tensor_scalar(tab[:, 0, :], grid[:], st[:, 6, 0:1], None, ALU.mult))
            then(V.tensor_scalar(tab[:, 1, :], tab[:, 0, :], -1.0, None, ALU.mult))
            then(V.tensor_tensor(tab[:, 2, :], tab[:, 0, :], tab[:, 1, :], ALU.max))
            then(V.tensor_scalar(tab[:, 3, :], tab[:, 2, :], st[:, 6, 1:2], 1e-6, ALU.mult, ALU.add))
            then(V.tensor_scalar(tab[:, 1, :], tab[:, 0, :], 0.0, None, ALU.mult))
            then(V.tensor_scalar(tab[:, 5, :], tab[:, 1, :], st[:, 8, 0:1], None, ALU.add))
            then(V.tensor_scalar(tab[:, 1, :], tab[:, 0, :], 0.0, None, ALU.is_lt))
            then(V.tensor_scalar(tab[:, 2, :], tab[:, 0, :], 0.0, None, ALU.is_gt))
            then(V.tensor_tensor(tab[:, 0, :], tab[:, 2, :], tab[:, 1, :], ALU.subtract))
            dve.wait_ge(c_pool, 1)
            then(V.tensor_tensor(tab[:, 2, :], tab[:, 0, :], tab[:, 4, :], ALU.mult))
            then(V.tensor_scalar(tab[:, 1, :], tab[:, 2, :], st[:, 9, 0:1], None, ALU.mult))
            dve.wait_ge(c_pe, 1)
            then(V.tensor_scalar(hidden[:, 0:TABLE], MI[0][:, 0:TABLE], cpbb1[:, 0:1], 0.0, ALU.add, ALU.max))
            dve.wait_ge(c_pe, 3)
            then(V.memset(tbs[:], 0.0))
            then(V.tensor_copy(tbs[:, 0, :], MI[1][0:TCH, 0:HEADS]))
            then(V.tensor_copy(tbs[0:TABLE - TCH, 1, :], MI[1][0:TABLE - TCH, 8:8 + HEADS]))
            dve.wait_ge(c_pe, 4)
            for v in range(4):
                t0, t1 = bias_t[:, 0, :], bias_t[:, 1, :]
                hi, mid, lo = (biasp[:, 3 * v + part, :] for part in range(3))
                then(V.tensor_tensor(t0.rearrange("q (h n) -> q h n", n=N), S[0][0:R, 0:HK].rearrange("q (h n) -> q h n", n=N),
                                     maskc[:, v, :].unsqueeze(1).broadcast_to([R, HEADS, N]), ALU.add))
                then(V.tensor_copy(hi, t0))
                then(V.tensor_tensor(t1, t0, hi, ALU.subtract))
                then(V.tensor_copy(mid, t1))
                then(V.tensor_tensor(lo, t1, mid, ALU.subtract))
            then(V.tensor_copy(identb[:], ident[:]))
            then(V.tensor_copy(identh[:], ident[:]))
            then(V.tensor_copy(headsel[:], headsel_f[:]))
            then(V.tensor_scalar(wqkv[:, 0:C], wqkv[:, 0:C], float(D) ** -0.5, None, ALU.mult))
            for b in range(2):
                then(V.memset(vx[b][:], 0.0))
                then(V.memset(vx[b][0:N, :, :, 2 * D:2 * D + 1], 1.0))
                then(V.memset(vx[b][W0:W0 + N, :, :, 2 * D + 1:2 * D + 2], 1.0))
            V.memset(O[:], 0.0).then_inc(c_ready, 1)
            dve.wait_ge(c_ready, 1)

            def statistics(src, stats_b, s_src, n_src, s_stat, s_y, u):
                dve.wait_ge(s_src, n_src)
                if later(u):
                    dve.wait_ge(s_stat, 9 * u)
                    dve.wait_ge(s_y, u)
                for p in range(PAIRS):
                    V.bn_stats(stats_b[:, p, :], src[:, p, :]).then_inc(s_stat, 1)

            def aggregate(stats_b, mv_b, veps_b, s_stat, s_rs_b, u):
                for p in range(PAIRS):
                    V.bn_aggr(mv_b[:, p, :], stats_b[:, p, :]).then_inc(s_stat, 1)
                dve.wait_ge(s_stat, 9 * u + 8)
                if later(u):
                    dve.wait_ge(s_rs_b, u)
                V.tensor_scalar(veps_b[:], mv_b[:, :, 1], EPS, None, ALU.add).then_inc(s_stat, 1)

            def ln_apply(src, mv_b, rstd_b, y_b, s_rs_b, s_y, s_used, u):
                dve.wait_ge(s_rs_b, u + 1)
                if later(u):
                    dve.wait_ge(s_used, u)
                for p in range(PAIRS):
                    ins = V.tensor_scalar(y_b[:, p, :], src[:, p, :], mv_b[:, p, 0:1], rstd_b[:, p:p + 1],
                                          ALU.subtract, ALU.mult)
                ins.then_inc(s_y, 1)

            def ln1_stats(u, b):
                statistics(xin[b], stats[b], s_x[b], 32 * u + 32, s_st[b], s_y0[b], u)

            def ln1_aggregate(u, b):
                aggregate(stats[b], mv[b], veps[b], s_st[b], s_rs[b], u)

            def ln1_apply(u, b):
                ln_apply(xin[b], mv[b], rstd[b], y0[b], s_rs[b], s_y0[b], s_y1[b], u)

            def ln2_stats(u, b):
                statistics(x1[b], stats2[b], s_x1[b], u + 1, s_st2[b], s_z0[b], u)

            def ln2_aggregate(u, b):
                aggregate(stats2[b], mv2[b], veps2[b], s_st2[b], s_rs2[b], u)

            def ln2_apply(u, b):
                ln_apply(x1[b], mv2[b], rstd2[b], z0[b], s_rs2[b], s_z0[b], s_z1[b], u)

            def low_parts(u, b):
                for h in range(2):
                    bank = MI[1 - h][0:R, 0:2 * 3 * C].rearrange("r (p f) -> r p f", p=2)
                    dve.wait_ge(s_vs[b], 2 * u + h + 1)
                    V.tensor_tensor(qkp[b][:, h::2, :, D:2 * D],
                                    bank[:, :, 0:2 * C].rearrange("r p (h d) -> r p h d", d=D),
                                    qkp[b][:, h::2, :, 0:D], ALU.subtract).then_inc(s_lo[b], 1)

            def repeat_parts(u, b):
                dve.wait_ge(s_lo[b], 2 * u + 2)
                q, k = qkp[b][:, :, 0:HEADS, :], qkp[b][:, :, HEADS:QKH, :]
                V.tensor_copy(q[:, :, :, 2 * D:4 * D], q[:, :, :, 0:2 * D]).then_inc(s_dup[b], 1)
                V.tensor_copy(k[:, :, :, 2 * D:3 * D], k[:, :, :, D:2 * D]).then_inc(s_dup[b], 1)
                V.tensor_copy(k[:, :, :, 3 * D:4 * D], k[:, :, :, 0:D]).then_inc(s_dup[b], 1)

            def place_qk(u, b):
                dve.wait_ge(s_qTp[b], u + 1)
                if later(u):
                    dve.wait_ge(s_sc, U * (u - 1) + 4 * b + 4)
                V.tensor_copy(qx[b][:].rearrange("c a n -> c (a n)"), MI[0][:, 0:4 * TP].bitcast(F16)).then_inc(s_qx[b], 1)
                dve.wait_ge(s_kTp[b], u + 1)
                for h in range(4):
                    rows = slice(HR * h, HR * h + HR)
                    V.tensor_copy(kx[b][rows, h].rearrange("c a n -> c (a n)"),
                                  MI[1][rows, 0:4 * TP].bitcast(F16)).then_inc(s_kx[b], 1)

            def place_v(u, b):
                dve.wait_ge(s_vs[b], 2 * u + 2)
                if later(u):
                    dve.wait_ge(s_pv, U * (u - 1) + 4 * b + 4)
                src = vs[b][:].rearrange("n p (h e d) -> n e p h d", h=4, e=2)
                dst = vx[b][:].rearrange("n (p w) h f -> n w p h f", w=2)
                for w in range(2):
                    for e in range(2):
                        V.tensor_copy(dst[W0 * e:W0 * e + N, w, :, :, D * e:D * e + D],
                                      src[W0 * w:W0 * w + N, e]).then_inc(s_vx[b], 1)

            def neg_max(u, j):
                n = U * u + j
                dve.wait_ge(s_sc, n + 1)
                if later(u) or j >= 2:
                    dve.wait_ge(s_nmp, n - 1)
                V.tensor_reduce(nm[j % 2][:], S[exp_bank(j)][0:R, 0:HK].rearrange("q (h n) -> q h n", n=N),
                                AX_X, ALU.max, negate=True).then_inc(s_nm, 1)

            def evac_nmT(u, j):
                n = U * u + j
                dve.wait_ge(s_nmp, n + 1)
                if later(u) or j >= 2:
                    dve.wait_ge(s_sh, n - 1)
                V.tensor_copy(nmT[j % 2][:, 0:R], PT[(j + 1) % 2][0:HEADS, NMT_COL:NMT_COL + 57].bitcast(BF16)[:, 0:R]
                              ).then_inc(s_nmT, 1)

            def evac_o(u, b):
                dve.wait_ge(s_pv, U * u + 4 * b + 4)
                if later(u):
                    dve.wait_ge(s_on[b], u)
                V.tensor_copy(o_sb[b][:], O[:, 0:T]).then_inc(s_o[b], 1)

            def recip(u, b):
                dve.wait_ge(s_den[b], u + 1)
                if later(u):
                    dve.wait_ge(s_on[b], u)
                V.reciprocal(rec[b][:], MI[b][:, 0:T]).then_inc(s_rec[b], 1)

            def add_attention(u, b):
                dve.wait_ge(s_pj[b], u + 1)
                dve.wait_ge(s_xres[b], u + 1)
                if later(u):
                    dve.wait_ge(s_x1b[b], u)
                    dve.wait_ge(s_z0[b], u)
                V.tensor_tensor(x1[b][:].rearrange("r p c -> r (p c)"), MI[0][0:R, 0:PAIRS * C],
                                xres[:, bass.ds((u % XRING) * 2 + b, 1), :].rearrange("r o f -> r (o f)"),
                                ALU.add).then_inc(s_x1[b], 1)

            def evac_zT(u, b):
                dve.wait_ge(s_zTp[b], u + 1)
                if later(u):
                    dve.wait_ge(s_f[b], 4 * u)
                V.tensor_copy(zT[b][:].rearrange("c (p w n) -> c p w n", p=2, w=2), zt_valid(b)).then_inc(s_zT[b], 1)

            def zt_valid(b):
                full = MI[1][:, 0:256].rearrange("c (p w n) -> c p w n", p=2, w=2)
                return full[:, :, :, 0:N]

            def evac_m(u, b):
                dve.wait_ge(s_m[b], u + 1)
                if later(u):
                    dve.wait_ge(s_mo[b], u)
                V.tensor_copy(mT[b][:, :, 0:N], MI[1][:, 0:T // 2].rearrange("c (w n) -> c w n", n=N)).then_inc(s_mT[b], 1)

            def result(u, b):
                dve.wait_ge(s_mo[b], u + 1)
                dve.wait_ge(s_x1b[b], u + 1)
                if later(u):
                    dve.wait_ge(s_out[b], 32 * u)
                V.tensor_tensor(res[b][:].rearrange("r p c -> r (p c)"), MI[0][0:R, 0:PAIRS * C],
                                x1b[b][:].rearrange("r p c -> r (p c)"), ALU.add).then_inc(s_res[b], 1)

            if NSB:
                ln1_stats(0, 0)

            def body(i):
                for k in range(U):
                    c, d, a = i - 1, i - 2, i + 1
                    if k == 0 and on_chip(a):
                        dve.wait_ge(s_st[0], 9 * a + 4)
                    if k == 2 and on_chip(a):
                        dve.wait_ge(s_st[1], 9 * a + 4)
                    if k == 2 and on_chip(c):
                        dve.wait_ge(s_st2[0], 9 * c + 4)
                    if k == 5 and on_chip(c):
                        dve.wait_ge(s_st2[1], 9 * c + 4)
                    u, j = at_unit(i, k, 1)
                    if on_chip(u):
                        evac_nmT(u, j)
                    if on_chip(i):
                        neg_max(i, k)
                    if k == 0 and on_chip(a):
                        ln1_aggregate(a, 0)
                    if k == 2 and on_chip(a):
                        ln1_aggregate(a, 1)
                    if k == 2 and on_chip(c):
                        ln2_aggregate(c, 0)
                    if k == 5 and on_chip(c):
                        ln2_aggregate(c, 1)
                    if k == 0:
                        if on_chip(c):
                            recip(c, 0)
                        if on_chip(d):
                            evac_m(d, 0)
                        if on_chip(i):
                            place_qk(i, 1)
                        if on_chip(a):
                            ln1_apply(a, 0)
                    if k == 1:
                        if on_chip(c):
                            add_attention(c, 0)
                        if on_chip(d):
                            evac_m(d, 1)
                            result(d, 0)
                        if on_chip(c):
                            ln2_stats(c, 0)
                        if on_chip(a):
                            ln1_stats(a, 1)
                    if k == 2:
                        if on_chip(c):
                            evac_o(c, 1)
                        if on_chip(d):
                            result(d, 1)
                        if on_chip(a):
                            low_parts(a, 0)
                        if on_chip(c):
                            ln2_apply(c, 0)
                        if on_chip(a):
                            ln1_apply(a, 1)
                    if k == 3:
                        if on_chip(c):
                            recip(c, 1)
                        if on_chip(a):
                            repeat_parts(a, 0)
                        if on_chip(i):
                            place_v(i, 1)
                    if k == 4:
                        if on_chip(a):
                            place_qk(a, 0)
                        if on_chip(c):
                            evac_zT(c, 0)
                            add_attention(c, 1)
                            ln2_stats(c, 1)
                    if k == 5:
                        if on_chip(a):
                            low_parts(a, 1)
                        if on_chip(c):
                            ln2_apply(c, 1)
                    if k == 6:
                        if on_chip(c):
                            evac_zT(c, 1)
                        if on_chip(i):
                            evac_o(i, 0)
                        if on_chip(a):
                            repeat_parts(a, 1)
                    if k == 7:
                        if on_chip(a):
                            place_v(a, 0)
                        if on_chip(i + 2):
                            ln1_stats(i + 2, 0)

            rounds(dve, body)

        @block.tensor
        def _(pe):
            MM = nc.tensor.matmul
            pe.wait_ge(c_in, 16 * N_IN)
            pe.wait_ge(c_chain, C_TAB)
            MM(MI[0][:, 0:TABLE], cpbw1[:], tab[:, 1, :], start=True, stop=True).then_inc(c_pe, 1)
            pe.wait_ge(c_chain, C_HID)
            for ch in range(2):
                rows = min(TCH, TABLE - ch * TCH)
                MM(MI[1][0:rows, 8 * ch:8 * ch + HEADS], hidden[:, ch * TCH:ch * TCH + rows], cpbw2[:],
                   start=True, stop=True).then_inc(c_pe, 1)
            pe.wait_ge(c_chain, C_TBS)
            for key in range(N):
                for ch in range(2):
                    mm = MM(S[0][0:R, 0:HK].rearrange("q (h n) -> q h n", n=N)[:, :, key], onehot[:, ch, key, :], tbs[:, ch, :],
                            start=(ch == 0), stop=(ch == 1))
            mm.then_inc(c_pe, 1)
            pe.wait_ge(c_ready, 1)
            pe.wait_ge(c_zero, ZEROED)

            def scores(u, j):
                n, b, p = U * u + j, j // 4, j % 4
                if later(u) or j >= 3:
                    pe.wait_ge(s_e, n + 1 - S_BACK[j])
                if p == 0:
                    pe.wait_ge(s_qx[b], u + 1)
                    pe.wait_ge(s_kx[b], 4 * (u + 1))
                bank = S[exp_bank(j)]
                row = ((u % 4) // 3) if b == 1 else 0
                for part in range(3):
                    if isinstance(row, int):
                        src = biasp[:, (2 * row + (p == 3)) * 3 + part, :]
                    else:
                        src = biasp[:, bass.ds(row * 6 + (p == 3) * 3 + part, 1), :].rearrange("q o f -> q (o f)")
                    MM(bank[0:R, 0:HK], identb[0:R, 0:R], src, start=(part == 0), stop=False, skip_group_check=True)
                for w in range(2):
                    t = W0 * w
                    for g in range(2):
                        mm = MM(bank[W0 * w:W0 * w + N, 4 * N * g:4 * N * (g + 1)], qx[b][:, 4 * g + p, t:t + N],
                                kx[b][:, :, 4 * g + p, t:t + N], start=False, stop=False, skip_group_check=True)
                mm.then_inc(s_sc, 1)

            def turn_max(u, j):
                n = U * u + j
                pe.wait_ge(s_nm, n + 1)
                if later(u) or j >= 3:
                    pe.wait_ge(s_pT, n - 2)
                nc.tensor.transpose(PT[(j + 1) % 2][0:HEADS, NMT_COL:NMT_COL + 57].bitcast(BF16)[:, 0:R], nm[j % 2][:],
                                    identb[0:R, 0:R]).then_inc(s_nmp, 1)

            def shift(u, j):
                n = U * u + j
                pe.wait_ge(s_nmT, n + 1)
                MM(S[exp_bank(j)][0:R, 0:HK], nmT[j % 2][:, 0:R], headsel[:], start=False, stop=True,
                   skip_group_check=True).then_inc(s_sh, 1)

            def turn_probs(u, j):
                n = U * u + j
                pe.wait_ge(s_e, n + 1)
                if later(u) or j >= 2:
                    pe.wait_ge(s_pT, n - 1)
                src = probs[j % 2][:].rearrange("q h n -> q (h n)")
                for hp in range(4):
                    mm = nc.tensor.transpose(PT[j % 2][0:R, R * hp:R * hp + R], src[:, 2 * W0 * hp:2 * W0 * hp + R],
                                             ident[0:R, 0:R])
                mm.then_inc(s_pTp, 1)

            def times_v(u, j):
                n, b, p = U * u + j, j // 4, j % 4
                pe.wait_ge(s_pT, n + 1)
                if p == 0:
                    pe.wait_ge(s_vx[b], 4 * u + 4)
                    if b == 1:
                        pe.wait_ge(s_o[0], u + 1)
                    elif later(u):
                        pe.wait_ge(s_o[1], u)
                for w in range(2):
                    for hp in range(4):
                        mm = MM(O[32 * hp:32 * hp + VC, (2 * p + w) * N:(2 * p + w + 1) * N], vx[b][:, 2 * p + w, hp, :],
                                pT[j % 2][:, hp, W0 * w:W0 * w + N], start=True, stop=True, tile_position=(0, 32 * hp))
                mm.then_inc(s_pv, 1)

            def turn_tokens(dst, src, cols, sem_out):
                tokens = src[:].rearrange("r p c -> r (p c)")
                for pp in range(2):
                    mm = nc.tensor.transpose(dst[:, cols * pp:cols * pp + R], tokens[:, 2 * C * pp:2 * C * pp + 2 * C],
                                             ident[0:R, 0:R])
                mm.then_inc(sem_out, 1)

            def turn_y(u, b):
                pe.wait_ge(s_y2[b], u + 1)
                turn_tokens(MI[Y_BANK[b]], y2[b], R, s_yTp[b])

            def turn_z(u, b):
                pe.wait_ge(s_z2[b], u + 1)
                turn_tokens(MI[1], z2[b], 128, s_zTp[b])

            def project_qkv(u, b, h):
                pe.wait_ge(s_yT[b], u + 1)
                rows = slice(C * h, C * h + C)
                for pp in range(2):
                    mm = MM(MI[1 - h][0:R, 3 * C * pp:3 * C * (pp + 1)], yT[b][rows, pp, 0:R], wqkv[rows, :],
                            start=True, stop=True)
                mm.then_inc(s_qkv[b], 1)

            def turn_qk(u, b, m):
                pe.wait_ge(s_dup[b], 3 * u + 3)
                dst = MI[m][:, 0:4 * TP].bitcast(F16).rearrange("c (a n) -> c a n", n=TP)
                src = qkp[b][:].rearrange("r p h f -> r p (h f)")
                for g in range(2):
                    for p in range(PAIRS):
                        first = (2 * m + g) * 4 * HR
                        mm = nc.tensor.transpose(dst[:, 4 * g + p, 0:R], src[:, p, first:first + 4 * HR], identh[0:R, 0:R])
                mm.then_inc((s_qTp, s_kTp)[m][b], 1)

            def spread_den(u, b):
                pe.wait_ge(s_o[b], u + 1)
                MM(MI[b][:, 0:T], densel[:], o_sb[b][:], start=True, stop=True).then_inc(s_den[b], 1)

            def project_out(u, b):
                pe.wait_ge(s_on[b], u + 1)
                src = on[b][:].rearrange("c w n -> c (w n)")
                for p in range(PAIRS):
                    mm = MM(MI[0][0:R, C * p:C * p + C], src[:, 2 * W0 * p:2 * W0 * p + R], wproj[:], start=True, stop=True)
                mm.then_inc(s_pj[b], 1)

            def fc1(u, b):
                pe.wait_ge(s_zT[b], u + 1)
                for n, (c, h) in enumerate(((0, 0), (1, 1), (0, 1), (1, 0))):
                    if n >= 2:
                        pe.wait_ge(s_f[b], 4 * u + n - 1)
                    rows = slice(C * h, C * h + C)
                    MM(MI[c][:, h * T // 2:(h + 1) * T // 2], w1[rows, 128 * c:128 * c + 128], zT[b][rows, :],
                       start=True, stop=True).then_inc(s_f[b], 1)

            def fc2(u, b):
                pe.wait_ge(s_g[b], 2 * u + 2)
                for h in range(2):
                    for c in range(2):
                        mm = MM(MI[1][C * h:C * h + C, 0:T // 2], w2[:, c, :], gl[b][:, c, h * T // 2:(h + 1) * T // 2],
                                start=(c == 0), stop=(c == 1), tile_position=(0, C * h))
                mm.then_inc(s_m[b], 1)

            def turn_back(u, b):
                pe.wait_ge(s_mT[b], u + 1)
                src = mT[b][:].rearrange("c w n -> c (w n)")
                for pp in range(2):
                    mm = nc.tensor.transpose(MI[0][0:R, 2 * C * pp:2 * C * pp + 2 * C], src[:, 2 * W0 * pp:2 * W0 * pp + R],
                                             ident[:])
                mm.then_inc(s_mo[b], 1)

            def after(*uses):
                for u, semaphore, count in uses:
                    if on_chip(u):
                        pe.wait_ge(semaphore, count)
                        return

            def body(i):
                for k in range(U):
                    if on_chip(i):
                        scores(i, k)
                    u1, j1 = at_unit(i, k, 1)
                    if on_chip(u1):
                        turn_max(u1, j1)
                    u3, j3 = at_unit(i, k, 3)
                    if on_chip(u3):
                        times_v(u3, j3)
                    if on_chip(u1):
                        shift(u1, j1)
                    u2, j2 = at_unit(i, k, 2)
                    if on_chip(u2):
                        turn_probs(u2, j2)
                    c, d = i - 1, i - 2
                    a = i + 1
                    den = [(c, s_rec[b], c + 1) for b in range(2)]
                    proj = [(c, s_x1[b], c + 1) for b in range(2)]
                    y = [(a, s_yT[b], a + 1) for b in range(2)]
                    qk = [(u, s_lo[b], 2 * u + 2) for u, b in ((a, 0), (a, 1), (i, 1))]
                    z = [(c, s_zT[b], c + 1) for b in range(2)]
                    fc = (c, s_g[0], 2 * c + 2), (d, s_g[1], 2 * d + 2)
                    mlp = [(d, s_mT[b], d + 1) for b in range(2)]
                    back = [(d, s_res[b], d + 1) for b in range(2)]
                    if k == 0:
                        if on_chip(c):
                            after(fc[1], qk[2])
                            spread_den(c, 0)
                        if on_chip(d):
                            after(fc[1])
                            fc2(d, 0)
                        if on_chip(i):
                            after(den[0], qk[2])
                            turn_qk(i, 1, 0)
                            after(mlp[0], qk[2])
                            turn_qk(i, 1, 1)
                    q1, k1 = (i, s_qx[1], i + 1), (i, s_kx[1], 4 * i + 4)
                    q0, k0 = (a, s_qx[0], a + 1), (a, s_kx[0], 4 * a + 4)
                    if k == 1:
                        if on_chip(c):
                            after(q1, den[0])
                            project_out(c, 0)
                        if on_chip(d):
                            after(k1, mlp[0])
                            fc2(d, 1)
                            after(proj[0], fc[1])
                            turn_back(d, 0)
                        if on_chip(a):
                            after(mlp[1], k1)
                            turn_y(a, 0)
                    if k == 2:
                        if on_chip(d):
                            after(back[0])
                            turn_back(d, 1)
                        if on_chip(a):
                            after(y[0])
                            project_qkv(a, 0, 0)
                            after(back[1], proj[0], q1)
                            project_qkv(a, 0, 1)
                    if k == 3:
                        if on_chip(c):
                            after(qk[0], mlp[1], k1)
                            spread_den(c, 1)
                    if k == 4:
                        if on_chip(a):
                            after(qk[0])
                            turn_qk(a, 0, 0)
                            after(den[1], qk[0])
                            turn_qk(a, 0, 1)
                            after(q0)
                            turn_y(a, 1)
                        if on_chip(c):
                            after(k0, den[1])
                            turn_z(c, 0)
                            after(y[1], back[1], proj[0])
                            project_out(c, 1)
                    if k == 5:
                        if on_chip(a):
                            after(z[0], k0)
                            project_qkv(a, 1, 0)
                            after(proj[1], y[1])
                            project_qkv(a, 1, 1)
                    if k == 6:
                        if on_chip(c):
                            after(qk[1], z[0])
                            turn_z(c, 1)
                    if k == 7:
                        if on_chip(c):
                            after(qk[1], proj[1])
                            pe.wait_ge(s_zT[1], c + 1)
                            fc1(c, 0)
                            after(fc[0])
                            fc1(c, 1)

            rounds(pe, body)


S_BANK = (0, 1, 2, 0, 1, 2, 0, 1)
Y_BANK = (1, 0)
S_BACK = (2, 2, 5, 3, 3, 3, 3, 3)


def shape_constants():
    ident = np.eye(128, dtype=np.float32)
    co = np.stack(np.meshgrid(np.arange(WIN), np.arange(WIN), indexing="ij")).reshape(2, -1)
    rel = co[:, :, None] - co[:, None, :]
    idx = (rel[0] + WIN - 1) * (2 * WIN - 1) + rel[1] + WIN - 1
    onehot = np.zeros((2 * TCH, N, R), np.float32)
    for q in range(N):
        for k in range(N):
            for w in range(2):
                onehot[idx[q, k], k, W0 * w + q] = 1.0
    onehot = np.ascontiguousarray(onehot.reshape(2, TCH, N, R))
    mask = np.zeros((R, 4, N), np.float32)
    part = np.where(np.arange(WIN) < WIN - SHIFT, 0, 1)
    for v in range(4):
        for w in range(2):
            rows = part[co[0]] * (v // 2)
            cols = part[co[1]] * (1 if v % 2 and w == 1 else 0)
            region = 2 * rows + cols
            mask[W0 * w:W0 * w + N, v] = np.where(region[:, None] != region[None, :], -1e9, 0.0)
    line = (np.arange(-(WIN - 1), WIN, dtype=np.float32) / np.float32(WIN - 1)).astype(np.float32)
    grid = np.stack(np.meshgrid(line, line, indexing="ij")).reshape(2, -1).astype(np.float32)
    headsel = np.zeros((HEADS, HEADS, N), np.float32)
    for h in range(HEADS):
        headsel[h, h] = 1.0
    densel = np.zeros((128, 128), np.float32)
    for m in range(128):
        densel[32 * (m // 32) + 2 * D + (1 if D <= m % 32 < 2 * D else 0), m] = 1.0
    return ident, onehot, mask, np.ascontiguousarray(grid), headsel.reshape(HEADS, HK), densel


def kernel(x, L0_conv_norm1_w, L0_conv_norm1_b, L0_conv_qkv_w, L0_conv_proj_w, L0_conv_proj_b, L0_conv_cpb_w1,
           L0_conv_cpb_b1, L0_conv_cpb_w2, L0_conv_h_times, L0_conv_pow_para, L0_conv_ws_scalar, L0_conv_ws_scalar2,
           L0_conv_norm2_w, L0_conv_norm2_b, L0_conv_fc1_w, L0_conv_fc1_b, L0_conv_fc2_w, L0_conv_fc2_b):
    import concourse.bacc as bacc
    from concourse.bass_utils import run_bass_kernel_spmd

    B, H, W, _ = x.shape
    nh, nw = H // WIN, W // WIN

    def rows(a):
        return np.broadcast_to(np.asarray(a).reshape(1, -1), (R, np.asarray(a).size))

    xs = np.roll(np.asarray(x), (-SHIFT, -SHIFT), axis=(1, 2))
    xs = xs.reshape(B, nh, WIN, PAIRS, 2, WIN, C).transpose(0, 1, 4, 2, 5, 3, 6).reshape(B * nh, 2, N, PAIRS, C)
    ident, onehot, mask, grid, headsel, densel = shape_constants()
    two = lambda a: np.broadcast_to(np.asarray(a).reshape(1, 1), (2, 1))
    fc2_wT = np.asarray(L0_conv_fc2_w).T.reshape(2, 128, C).transpose(1, 0, 2)
    ins = {
        "x": xs, "norm1_w": rows(L0_conv_norm1_w), "norm1_b": rows(L0_conv_norm1_b),
        "qkv_wT": np.asarray(L0_conv_qkv_w).T, "proj_wT": np.asarray(L0_conv_proj_w).T, "proj_b": rows(L0_conv_proj_b),
        "cpb_w1T": np.asarray(L0_conv_cpb_w1).T, "cpb_b1": np.asarray(L0_conv_cpb_b1).reshape(-1, 1),
        "cpb_w2T": np.asarray(L0_conv_cpb_w2).T, "h_times": two(L0_conv_h_times), "pow_para": two(L0_conv_pow_para),
        "ws_scalar": two(L0_conv_ws_scalar), "ws_scalar2": two(L0_conv_ws_scalar2),
        "norm2_w": rows(L0_conv_norm2_w), "norm2_b": rows(L0_conv_norm2_b), "fc1_wT": np.asarray(L0_conv_fc1_w).T,
        "fc1_b": np.asarray(L0_conv_fc1_b).reshape(2, 128).T, "fc2_wT": fc2_wT, "fc2_b": rows(L0_conv_fc2_b),
        "c_ident": ident, "c_onehot": onehot, "c_mask": mask, "c_grid": grid, "c_headsel": headsel, "c_densel": densel,
    }
    nc = bacc.Bacc("TRN2", target_bir_lowering=False, num_devices=1)
    arrays, aps = {}, {}
    for name, a in ins.items():
        a = np.ascontiguousarray(a)
        arrays["in_" + name] = a
        aps[name] = nc.dram_tensor("in_" + name, a.shape, mybir.dt.from_np(a.dtype), kind="ExternalInput").ap()
    out = nc.dram_tensor("out", xs.shape, F32, kind="ExternalOutput").ap()
    swin_block(nc, out=out, **aps)
    r = run_bass_kernel_spmd(nc, [arrays], core_ids=[0])
    got = r.results[0]["out"]
    got = got.reshape(B, nh, 2, WIN, WIN, PAIRS, C).transpose(0, 1, 3, 5, 2, 4, 6).reshape(B, H, W, C)
    return np.roll(got, (SHIFT, SHIFT), axis=(1, 2))
```

```python
from contextlib import ExitStack

import numpy as np

import concourse.bass as bass
from concourse import mybir

F32 = mybir.dt.float32
BF16 = mybir.dt.bfloat16
F16 = mybir.dt.float16
ACT = mybir.ActivationFunctionType
ALU = mybir.AluOpType
AX_X = mybir.AxisListType.X

WIN = 7
N = WIN * WIN
SHIFT = 3
HEADS = 8
D = 8
C = HEADS * D
HID = 4 * C
PAIRS = 4
W0 = 64
R = W0 + N
T = PAIRS * 2 * N
HK = HEADS * N
QKH = 2 * HEADS
HR = 32
TP = R + 1
TABLE = (2 * WIN - 1) ** 2
TCH = (TABLE + 1) // 2
VC = 2 * D + 2
EPS = 1e-5
U = 8
XRING = 4


def swin_block(nc, x, norm1_w, norm1_b, qkv_wT, proj_wT, proj_b, cpb_w1T, cpb_b1, cpb_w2T, h_times,
               pow_para, ws_scalar, ws_scalar2, norm2_w, norm2_b, fc1_wT, fc1_b, fc2_wT, fc2_b,
               c_ident, c_onehot, c_mask, c_grid, c_headsel, out):
    NB = x.shape[0]
    NSB = NB // 2
    ctx = ExitStack()
    with ctx:
        def sb(name, shape, dt=F32):
            return ctx.enter_context(nc.sbuf_tensor(name, shape, dt))

        def ps(name):
            return ctx.enter_context(nc.psum_tensor(name, [128, 512], F32))

        def sem(name):
            return ctx.enter_context(nc.semaphore(name))

        ident = sb("ident", [128, 128])
        identb = sb("identb", [128, 128], BF16)
        identh = sb("identh", [128, 128], F16)
        onehot = sb("onehot", [TCH, 2, N, R])
        maskc = sb("maskc", [R, 4, N])
        grid = sb("grid", [2, TABLE])
        headsel_f = sb("headsel_f", [HEADS, HK])
        headsel = sb("headsel", [HEADS, HK], BF16)
        n1w, n1b, n2w, n2b, fc2b = (sb(name, [2 * C, 1]) for name in ("n1w", "n1b", "n2w", "n2b", "fc2b"))
        projb = sb("projb", [R, C])
        wqkv = sb("wqkv", [2 * C, 3 * C])
        wproj = sb("wproj", [2 * C, 2 * C])
        w1 = sb("w1", [2 * C, HID])
        w2 = sb("w2", [128, 2, C])
        b1 = sb("b1", [128, 2])
        cpbw1 = sb("cpbw1", [2, 128])
        cpbb1 = sb("cpbb1", [128, 1])
        cpbw2 = sb("cpbw2", [128, HEADS])
        scal = sb("scal", [2, 4])
        st = sb("st", [2, 12, 4])
        tab = sb("tab", [2, 6, TABLE])
        hidden = sb("hidden", [128, 2 * TCH])
        tbs = sb("tbs", [TCH, 2, HEADS])
        mhalf = sb("mhalf", [R, PAIRS])
        bias_t = sb("bias_t", [R, 2, HK])
        biasp = sb("biasp", [R, 4 * 3, HK], BF16)

        xin = [sb(f"xin{b}", [R, PAIRS, C]) for b in range(2)]
        xres = sb("xres", [R, XRING * 2, PAIRS * C])
        stats = [sb(f"stats{b}", [R, PAIRS, 6]) for b in range(2)]
        mv = [sb(f"mv{b}", [R, PAIRS, 2]) for b in range(2)]
        veps = [sb(f"veps{b}", [R, PAIRS]) for b in range(2)]
        rstd = [sb(f"rstd{b}", [R, PAIRS]) for b in range(2)]
        y0 = [sb(f"y0{b}", [R, PAIRS, C]) for b in range(2)]
        y1 = [sb(f"y1{b}", [R, PAIRS, C]) for b in range(2)]
        yT = [sb(f"yT{b}", [2 * C, 2, 128]) for b in range(2)]
        qkp = [sb(f"qkp{b}", [R, PAIRS, QKH, HR], F16) for b in range(2)]
        vs = [sb(f"vs{b}", [R, PAIRS, C]) for b in range(2)]
        qx = [sb(f"qx{b}", [128, 2 * PAIRS, TP], F16) for b in range(2)]
        kx = [sb(f"kx{b}", [128, 4, 2 * PAIRS, TP], F16) for b in range(2)]
        vx = [sb(f"vx{b}", [R, 2 * PAIRS, 4, VC]) for b in range(2)]
        nm = [sb(f"nm{n}", [R, HEADS], BF16) for n in range(2)]
        nmT = [sb(f"nmT{n}", [HEADS, 114], BF16) for n in range(2)]
        probs = [sb(f"probs{n}", [R, HEADS, W0]) for n in range(2)]
        pT = [sb(f"pT{n}", [R, 4, R]) for n in range(2)]
        rec = [sb(f"rec{b}", [R, 4 * PAIRS, 2]) for b in range(2)]
        on = [sb(f"on{b}", [R, PAIRS, C]) for b in range(2)]
        oT = [sb(f"oT{b}", [2 * C, 2, 128]) for b in range(2)]
        stats2 = [sb(f"stats2{b}", [R, PAIRS, 6]) for b in range(2)]
        mv2 = [sb(f"mv2{b}", [R, PAIRS, 2]) for b in range(2)]
        veps2 = [sb(f"veps2{b}", [R, PAIRS]) for b in range(2)]
        rstd2 = [sb(f"rstd2{b}", [R, PAIRS]) for b in range(2)]
        z0 = [sb(f"z0{b}", [R, PAIRS, C]) for b in range(2)]
        z1 = [sb(f"z1{b}", [R, PAIRS, C]) for b in range(2)]
        zT = [sb(f"zT{b}", [2 * C, T // 2]) for b in range(2)]
        gl = [sb(f"gl{b}", [128, 2, T]) for b in range(2)]
        mT = [sb(f"mT{b}", [2 * C, PAIRS, W0]) for b in range(2)]
        res = [sb(f"res{b}", [R, PAIRS, C]) for b in range(2)]

        S = [ps(f"S{n}") for n in range(2)]
        PT = ps("PT")
        O = ps("O")
        M = [ps(f"M{n}") for n in range(4)]
        NMT_COL = PAIRS * 4 * VC

        c_in = sem("c_in")
        c_zero = sem("c_zero")
        c_chain = sem("c_chain")
        c_ready = sem("c_ready")
        c_act = sem("c_act")
        c_pool = sem("c_pool")
        c_pe = sem("c_pe")
        s_x = [sem(f"s_x{b}") for b in range(2)]
        s_st = [sem(f"s_st{b}") for b in range(2)]
        s_rs = [sem(f"s_rs{b}") for b in range(2)]
        s_y0 = [sem(f"s_y0{b}") for b in range(2)]
        s_y1 = [sem(f"s_y1{b}") for b in range(2)]
        s_xres = [sem(f"s_xres{b}") for b in range(2)]
        s_yTp = [sem(f"s_yTp{b}") for b in range(2)]
        s_yT = [sem(f"s_yT{b}") for b in range(2)]
        s_qkv = [sem(f"s_qkv{b}") for b in range(2)]
        s_hi = [sem(f"s_hi{b}") for b in range(2)]
        s_vs = [sem(f"s_vs{b}") for b in range(2)]
        s_lo = [sem(f"s_lo{b}") for b in range(2)]
        s_dup = [sem(f"s_dup{b}") for b in range(2)]
        s_qTp = [sem(f"s_qTp{b}") for b in range(2)]
        s_kTp = [sem(f"s_kTp{b}") for b in range(2)]
        s_qx = [sem(f"s_qx{b}") for b in range(2)]
        s_kx = [sem(f"s_kx{b}") for b in range(2)]
        s_kx3 = [sem(f"s_kx3{b}") for b in range(2)]
        s_vx = [sem(f"s_vx{b}") for b in range(2)]
        s_sc = sem("s_sc")
        s_nm = sem("s_nm")
        s_nmp = sem("s_nmp")
        s_nmT = sem("s_nmT")
        s_sh = sem("s_sh")
        s_e = sem("s_e")
        s_pTp = sem("s_pTp")
        s_pT = sem("s_pT")
        s_pv = sem("s_pv")
        s_rec = [sem(f"s_rec{b}") for b in range(2)]
        s_on = [sem(f"s_on{b}") for b in range(2)]
        s_oTp = [sem(f"s_oTp{b}") for b in range(2)]
        s_oT = [sem(f"s_oT{b}") for b in range(2)]
        s_pj = [sem(f"s_pj{b}") for b in range(2)]
        s_x1 = [sem(f"s_x1{b}") for b in range(2)]
        s_st2 = [sem(f"s_st2{b}") for b in range(2)]
        s_rs2 = [sem(f"s_rs2{b}") for b in range(2)]
        s_z0 = [sem(f"s_z0{b}") for b in range(2)]
        s_z1 = [sem(f"s_z1{b}") for b in range(2)]
        s_zTp = [sem(f"s_zTp{b}") for b in range(2)]
        s_zT = [sem(f"s_zT{b}") for b in range(2)]
        s_f = [sem(f"s_f{b}") for b in range(2)]
        s_g = [sem(f"s_g{b}") for b in range(2)]
        s_m = [sem(f"s_m{b}") for b in range(2)]
        s_mT = [sem(f"s_mT{b}") for b in range(2)]
        s_mo = [sem(f"s_mo{b}") for b in range(2)]
        s_res = [sem(f"s_res{b}") for b in range(2)]
        s_out = [sem(f"s_out{b}") for b in range(2)]

        N_IN = 27
        ZEROED = 12
        C_ABS, C_POW, C_TAB, C_HID, C_TBS = 3, 13, 18, 19, 22

        def on_chip(u):
            return not isinstance(u, int) or 0 <= u < NSB

        def later(u, k=1):
            return not isinstance(u, int) or u >= k

        def rounds(eng, body):
            for i in range(-1, 3):
                body(i)
            with eng.Fori(3, NSB - 2) as i:
                body(i)
            for i in range(NSB - 2, NSB + 2):
                body(i)

        def at_unit(i, k, back):
            return i + (k - back) // U, (k - back) % U

        def resid(u, b):
            return xres[:, bass.ds((u % XRING) * 2 + b, 1), :].rearrange("r o (p c) -> r (o p) c", p=PAIRS)

        block = ctx.enter_context(nc.Block())

        @block.sync
        def _(sp):
            ins = [(ident[:], c_ident), (onehot[:, 0], c_onehot[0]), (onehot[:, 1], c_onehot[1]),
                   (maskc[:], c_mask), (grid[:], c_grid), (headsel_f[:], c_headsel),
                   (n1w[:], norm1_w), (n1b[:], norm1_b), (n2w[:], norm2_w), (n2b[:], norm2_b),
                   (projb[:], proj_b), (fc2b[:], fc2_b), (wqkv[0:C], qkv_wT), (wqkv[C:2 * C], qkv_wT), (w1[0:C], fc1_wT),
                   (w1[C:2 * C], fc1_wT),
                   (w2[:], fc2_wT), (b1[:], fc1_b), (cpbw1[:], cpb_w1T), (cpbb1[:], cpb_b1),
                   (cpbw2[:], cpb_w2T), (scal[:, 0:1], h_times), (scal[:, 1:2], ws_scalar),
                   (scal[:, 2:3], ws_scalar2), (scal[:, 3:4], pow_para)]
            for dst, src in ins:
                sp.dma_start(dst, src).then_inc(c_in, 16)
            sp.wait_ge(c_zero, 1)
            for h in range(2):
                sp.dma_start(wproj[C * h:C * h + C, C * h:C * h + C], proj_wT).then_inc(c_in, 16)
            sp.wait_ge(c_zero, ZEROED)

            def load(u, b):
                src = [x[2 * u + b, w] for w in range(2)]
                if later(u):
                    sp.wait_ge(s_y0[b], u)
                    sp.wait_ge(s_xres[b], u)
                for w in range(2):
                    sp.dma_start(xin[b][W0 * w:W0 * w + N], src[w]).then_inc(s_x[b], 16)

            def store(u, b):
                sp.wait_ge(s_res[b], u + 1)
                for w in range(2):
                    sp.dma_start(out[2 * u + b, w], res[b][W0 * w:W0 * w + N]).then_inc(s_out[b], 16)

            load(0, 0)
            load(0, 1)

            def body(i):
                if on_chip(i + 2):
                    load(i + 2, 0)
                if on_chip(i - 2):
                    store(i - 2, 0)
                    store(i - 2, 1)
                if on_chip(i + 2):
                    load(i + 2, 1)

            rounds(sp, body)
            for b in range(2):
                sp.wait_ge(s_out[b], 32 * NSB)

        @block.gpsimd
        def _(pool):
            nc.gpsimd.memset(wproj[:], 0.0).then_inc(c_zero, 1)
            for b in range(2):
                nc.gpsimd.memset(xin[b][:], 0.0).then_inc(c_zero, 1)
                nc.gpsimd.memset(kx[b][:], 0.0).then_inc(c_zero, 1)
                nc.gpsimd.memset(mT[b][:], 0.0).then_inc(c_zero, 1)
                nc.gpsimd.memset(probs[b][:], 0.0).then_inc(c_zero, 1)
                nc.gpsimd.memset(nmT[b][:], 0.0).then_inc(c_zero, 1)
            nc.gpsimd.memset(mhalf[:], -0.5).then_inc(c_zero, 1)
            pool.wait_ge(c_zero, ZEROED)
            pool.wait_ge(c_chain, C_POW)
            nc.gpsimd.tensor_tensor(tab[:, 4, :], tab[:, 3, :], tab[:, 5, :], ALU.pow).then_inc(c_pool, 1)

            def ln_rstd(veps_b, rstd_b, s_veps, s_rs_b, u, s_used):
                pool.wait_ge(s_veps, 9 * u + 9)
                if later(u):
                    pool.wait_ge(s_used, u)
                nc.gpsimd.tensor_tensor(rstd_b[:], veps_b[:], mhalf[:], ALU.pow).then_inc(s_rs_b, 1)

            def normalise_rows(src, mv_b, rstd_b, a0, a1, s_rs_b, s0, s1, s_used, u):
                pool.wait_ge(s_rs_b, u + 1)
                if later(u):
                    pool.wait_ge(s1, u)
                nc.gpsimd.tensor_tensor(a0[:], src, mv_b[:, :, 0:1].broadcast_to([R, PAIRS, C]), ALU.subtract).then_inc(s0, 1)
                pool.wait_ge(s0, u + 1)
                if later(u):
                    pool.wait_ge(s_used, u)
                nc.gpsimd.tensor_tensor(a1[:], a0[:], rstd_b[:].unsqueeze(2).broadcast_to([R, PAIRS, C]),
                                        ALU.mult).then_inc(s1, 1)

            def keep_residual(u, b):
                if later(u, XRING):
                    pool.wait_ge(s_res[b], u - XRING + 1)
                pool.wait_ge(s_x[b], 32 * u + 32)
                nc.gpsimd.tensor_tensor(resid(u, b), xin[b][:], projb[:].unsqueeze(1).broadcast_to([R, PAIRS, C]),
                                        ALU.add).then_inc(s_xres[b], 1)

            def ln1_rstd(u, b):
                ln_rstd(veps[b], rstd[b], s_st[b], s_rs[b], u, s_y1[b])

            def ln2_rstd(u, b):
                ln_rstd(veps2[b], rstd2[b], s_st2[b], s_rs2[b], u, s_z1[b])

            def ln1_rows(u, b):
                normalise_rows(xin[b][:], mv[b], rstd[b], y0[b], y1[b], s_rs[b], s_y0[b], s_y1[b], s_yTp[b], u)

            def ln2_rows(u, b):
                normalise_rows(resid(u, b), mv2[b], rstd2[b], z0[b], z1[b], s_rs2[b], s_z0[b], s_z1[b], s_zTp[b], u)

            def body(i):
                c, a = i - 1, i + 1
                if on_chip(c):
                    ln2_rstd(c, 0)
                if on_chip(a):
                    ln1_rstd(a, 0)
                    ln1_rows(a, 0)
                if on_chip(c):
                    ln2_rows(c, 0)
                if on_chip(a):
                    keep_residual(a, 0)
                if on_chip(c):
                    ln2_rstd(c, 1)
                    ln2_rows(c, 1)
                if on_chip(a):
                    ln1_rstd(a, 1)
                    ln1_rows(a, 1)
                    keep_residual(a, 1)

            rounds(pool, body)

        @block.scalar
        def _(act):
            act.wait_ge(c_chain, C_ABS)
            nc.scalar.activation(st[:, 2, 0:3], st[:, 1, 0:3], ACT.Exp, scale=-1.0).then_inc(c_act, 1)
            nc.scalar.activation(st[:, 3, 0:1], scal[:, 3:4], ACT.Exp, scale=-1.0).then_inc(c_act, 1)
            act.wait_ge(c_act, 2)
            nc.scalar.activation(st[:, 4, 0:3], st[:, 2, 0:3], ACT.Ln, bias=1.0).then_inc(c_act, 1)

            def evac_yT(u, b):
                act.wait_ge(s_yTp[b], u + 1)
                if later(u):
                    act.wait_ge(s_qkv[b], 2 * u)
                nc.scalar.activation(yT[b][:, :, 0:R], M[0][:, 0:2 * R].rearrange("c (p r) -> c p r", p=2),
                                     ACT.Identity, bias=n1b[:, 0:1], scale=n1w[:, 0:1]).then_inc(s_yT[b], 1)

            def evac_oT(u, b):
                act.wait_ge(s_oTp[b], u + 1)
                if later(u):
                    act.wait_ge(s_pj[b], u)
                nc.scalar.activation(oT[b][:, :, 0:R], M[1][:, 0:2 * R].rearrange("c (p r) -> c p r", p=2),
                                     ACT.Copy).then_inc(s_oT[b], 1)

            def keep_qkv(u, b):
                for h in range(2):
                    bank = M[h][0:R, 0:2 * 3 * C].rearrange("r (p f) -> r p f", p=2)
                    act.wait_ge(s_qkv[b], 2 * u + h + 1)
                    if later(u):
                        act.wait_ge(s_kTp[b], u)
                        act.wait_ge(s_vx[b], 4 * u)
                    nc.scalar.activation(qkp[b][:, h::2, :, 0:D],
                                         bank[:, :, 0:2 * C].rearrange("r p (h d) -> r p h d", d=D),
                                         ACT.Copy).then_inc(s_hi[b], 1)
                    nc.scalar.activation(vs[b][:, h::2, :], bank[:, :, 2 * C:3 * C], ACT.Copy).then_inc(s_vs[b], 1)

            def place_qk(u, b):
                act.wait_ge(s_qTp[b], u + 1)
                if later(u):
                    act.wait_ge(s_sc, U * (u - 1) + 4 * b + 4)
                nc.scalar.activation(qx[b][:].rearrange("c a n -> c (a n)"), M[0][:, 0:4 * TP].bitcast(F16),
                                     ACT.Copy).then_inc(s_qx[b], 1)
                act.wait_ge(s_kTp[b], u + 1)
                rows = slice(3 * HR, 4 * HR)
                nc.scalar.activation(kx[b][rows, 3].rearrange("c a n -> c (a n)"), M[1][rows, 0:4 * TP].bitcast(F16),
                                     ACT.Copy).then_inc(s_kx3[b], 1)

            def exp(u, j):
                n = U * u + j
                act.wait_ge(s_sh, n + 1)
                if later(u) or j >= 2:
                    act.wait_ge(s_pTp, n - 1)
                nc.scalar.activation(probs[j % 2][:, :, 0:N], S[j % 2][0:R, 0:HK].rearrange("q (h n) -> q h n", n=N),
                                     ACT.Exp).then_inc(s_e, 1)

            def evac_pT(u, j):
                n = U * u + j
                act.wait_ge(s_pTp, n + 1)
                if later(u) or j >= 2:
                    act.wait_ge(s_pv, n - 1)
                nc.scalar.activation(pT[j % 2][:].rearrange("k h r -> k (h r)"), PT[0:R, 0:4 * R],
                                     ACT.Copy).then_inc(s_pT, 1)

            def gelu(u, b):
                for c in range(2):
                    act.wait_ge(s_f[b], 4 * u + 3 + c)
                    if later(u):
                        act.wait_ge(s_m[b], u)
                    nc.scalar.activation(gl[b][:, c, :], M[FC_BANK[b] + c][:, 0:T], ACT.Gelu,
                                         bias=b1[:, c:c + 1]).then_inc(s_g[b], 1)

            def body(i):
                c, a = i - 1, i + 1
                for k in range(U):
                    u, j = at_unit(i, k, 1)
                    if on_chip(u):
                        exp(u, j)
                    u, j = at_unit(i, k, 2)
                    if on_chip(u):
                        evac_pT(u, j)
                    if k == 0 and on_chip(i):
                        keep_qkv(i, 1)
                    if k == 2 and on_chip(i):
                        place_qk(i, 1)
                    if k == 3:
                        if on_chip(c):
                            evac_oT(c, 1)
                        if on_chip(a):
                            evac_yT(a, 0)
                    if k == 4 and on_chip(a):
                        keep_qkv(a, 0)
                    if k == 6 and on_chip(a):
                        place_qk(a, 0)
                    if k == 7:
                        if on_chip(a):
                            evac_yT(a, 1)
                        if on_chip(i):
                            evac_oT(i, 0)
                        if on_chip(c):
                            gelu(c, 0)
                            gelu(c, 1)

            rounds(act, body)

        @block.vector
        def _(dve):
            steps = [0]

            def then(ins):
                steps[0] += 1
                ins.then_inc(c_chain, 1)
                dve.wait_ge(c_chain, steps[0])

            V = nc.vector
            dve.wait_ge(c_in, 16 * N_IN)
            then(V.tensor_scalar(st[:, 0, 0:3], scal[:, 0:3], -1.0, None, ALU.mult))
            then(V.tensor_tensor(st[:, 1, 0:3], scal[:, 0:3], st[:, 0, 0:3], ALU.max))
            then(V.tensor_scalar(st[:, 5, 0:3], scal[:, 0:3], 0.0, None, ALU.max))
            dve.wait_ge(c_act, 3)
            then(V.tensor_tensor(st[:, 6, 0:3], st[:, 5, 0:3], st[:, 4, 0:3], ALU.add))
            then(V.tensor_scalar(st[:, 7, 0:1], st[:, 3, 0:1], 1.0, None, ALU.add))
            then(V.reciprocal(st[:, 8, 0:1], st[:, 7, 0:1]))
            then(V.reciprocal(st[:, 9, 0:1], st[:, 6, 2:3]))
            then(V.tensor_scalar(tab[:, 0, :], grid[:], st[:, 6, 0:1], None, ALU.mult))
            then(V.tensor_scalar(tab[:, 1, :], tab[:, 0, :], -1.0, None, ALU.mult))
            then(V.tensor_tensor(tab[:, 2, :], tab[:, 0, :], tab[:, 1, :], ALU.max))
            then(V.tensor_scalar(tab[:, 3, :], tab[:, 2, :], st[:, 6, 1:2], 1e-6, ALU.mult, ALU.add))
            then(V.tensor_scalar(tab[:, 1, :], tab[:, 0, :], 0.0, None, ALU.mult))
            then(V.tensor_scalar(tab[:, 5, :], tab[:, 1, :], st[:, 8, 0:1], None, ALU.add))
            then(V.tensor_scalar(tab[:, 1, :], tab[:, 0, :], 0.0, None, ALU.is_lt))
            then(V.tensor_scalar(tab[:, 2, :], tab[:, 0, :], 0.0, None, ALU.is_gt))
            then(V.tensor_tensor(tab[:, 0, :], tab[:, 2, :], tab[:, 1, :], ALU.subtract))
            dve.wait_ge(c_pool, 1)
            then(V.tensor_tensor(tab[:, 2, :], tab[:, 0, :], tab[:, 4, :], ALU.mult))
            then(V.tensor_scalar(tab[:, 1, :], tab[:, 2, :], st[:, 9, 0:1], None, ALU.mult))
            dve.wait_ge(c_pe, 1)
            then(V.tensor_scalar(hidden[:, 0:TABLE], M[0][:, 0:TABLE], cpbb1[:, 0:1], 0.0, ALU.add, ALU.max))
            dve.wait_ge(c_pe, 3)
            then(V.memset(tbs[:], 0.0))
            then(V.tensor_copy(tbs[:, 0, :], M[1][0:TCH, 0:HEADS]))
            then(V.tensor_copy(tbs[0:TABLE - TCH, 1, :], M[1][0:TABLE - TCH, 8:8 + HEADS]))
            dve.wait_ge(c_pe, 4)
            for v in range(4):
                t0, t1 = bias_t[:, 0, :], bias_t[:, 1, :]
                hi, mid, lo = (biasp[:, 3 * v + part, :] for part in range(3))
                then(V.tensor_tensor(t0.rearrange("q (h n) -> q h n", n=N), S[0][0:R, 0:HK].rearrange("q (h n) -> q h n", n=N),
                                     maskc[:, v, :].unsqueeze(1).broadcast_to([R, HEADS, N]), ALU.add))
                then(V.tensor_copy(hi, t0))
                then(V.tensor_tensor(t1, t0, hi, ALU.subtract))
                then(V.tensor_copy(mid, t1))
                then(V.tensor_tensor(lo, t1, mid, ALU.subtract))
            then(V.tensor_copy(identb[:], ident[:]))
            then(V.tensor_copy(identh[:], ident[:]))
            then(V.tensor_copy(headsel[:], headsel_f[:]))
            then(V.tensor_scalar(wqkv[:, 0:C], wqkv[:, 0:C], float(D) ** -0.5, None, ALU.mult))
            for b in range(2):
                then(V.memset(vx[b][:], 0.0))
                then(V.memset(vx[b][0:N, :, :, 2 * D:2 * D + 1], 1.0))
                then(V.memset(vx[b][W0:W0 + N, :, :, 2 * D + 1:2 * D + 2], 1.0))
            V.memset(O[:], 1.0).then_inc(c_ready, 1)
            dve.wait_ge(c_ready, 1)

            def statistics(src, stats_b, s_stat):
                for p in range(PAIRS):
                    V.bn_stats(stats_b[:, p, :], src[:, p, :]).then_inc(s_stat, 1)

            def aggregate(stats_b, mv_b, s_stat):
                for p in range(PAIRS):
                    V.bn_aggr(mv_b[:, p, :], stats_b[:, p, :]).then_inc(s_stat, 1)

            def add_eps(mv_b, veps_b, s_stat, s_rs_b, u):
                dve.wait_ge(s_stat, 9 * u + 8)
                if later(u):
                    dve.wait_ge(s_rs_b, u)
                V.tensor_scalar(veps_b[:], mv_b[:, :, 1], EPS, None, ALU.add).then_inc(s_stat, 1)

            def ln1_stats(u, b):
                dve.wait_ge(s_x[b], 32 * u + 32)
                if later(u):
                    dve.wait_ge(s_y0[b], u)
                statistics(xin[b], stats[b], s_st[b])

            def ln1_aggregate(u, b):
                aggregate(stats[b], mv[b], s_st[b])

            def ln1_eps(u, b):
                add_eps(mv[b], veps[b], s_st[b], s_rs[b], u)

            def ln2_stats_ready(u, b):
                dve.wait_ge(s_x1[b], u + 1)
                if later(u):
                    dve.wait_ge(s_z0[b], u)

            def ln2_stats(u, b):
                statistics(resid(u, b), stats2[b], s_st2[b])

            def ln2_aggregate(u, b):
                aggregate(stats2[b], mv2[b], s_st2[b])
                add_eps(mv2[b], veps2[b], s_st2[b], s_rs2[b], u)

            def low_parts(u, b):
                for h in range(2):
                    bank = M[h][0:R, 0:2 * 3 * C].rearrange("r (p f) -> r p f", p=2)
                    dve.wait_ge(s_vs[b], 2 * u + h + 1)
                    V.tensor_tensor(qkp[b][:, h::2, :, D:2 * D],
                                    bank[:, :, 0:2 * C].rearrange("r p (h d) -> r p h d", d=D),
                                    qkp[b][:, h::2, :, 0:D], ALU.subtract).then_inc(s_lo[b], 1)

            def repeat_parts(u, b):
                dve.wait_ge(s_lo[b], 2 * u + 2)
                q, k = qkp[b][:, :, 0:HEADS, :], qkp[b][:, :, HEADS:QKH, :]
                V.tensor_copy(q[:, :, :, 2 * D:4 * D], q[:, :, :, 0:2 * D]).then_inc(s_dup[b], 1)
                V.tensor_copy(k[:, :, :, 2 * D:3 * D], k[:, :, :, D:2 * D]).then_inc(s_dup[b], 1)
                V.tensor_copy(k[:, :, :, 3 * D:4 * D], k[:, :, :, 0:D]).then_inc(s_dup[b], 1)

            def place_k(u, b):
                dve.wait_ge(s_kTp[b], u + 1)
                if later(u):
                    dve.wait_ge(s_sc, U * (u - 1) + 4 * b + 4)
                for h in range(3):
                    rows = slice(HR * h, HR * h + HR)
                    V.tensor_copy(kx[b][rows, h].rearrange("c a n -> c (a n)"),
                                  M[1][rows, 0:4 * TP].bitcast(F16)).then_inc(s_kx[b], 1)

            def place_v(u, b):
                dve.wait_ge(s_vs[b], 2 * u + 2)
                if later(u):
                    dve.wait_ge(s_pv, U * (u - 1) + 4 * b + 4)
                src = vs[b][:].rearrange("n p (h e d) -> n e p h d", h=4, e=2)
                dst = vx[b][:].rearrange("n (p w) h f -> n w p h f", w=2)
                for w in range(2):
                    for e in range(2):
                        V.tensor_copy(dst[W0 * e:W0 * e + N, w, :, :, D * e:D * e + D],
                                      src[W0 * w:W0 * w + N, e]).then_inc(s_vx[b], 1)

            def neg_max(u, j):
                n = U * u + j
                dve.wait_ge(s_sc, n + 1)
                if later(u) or j >= 2:
                    dve.wait_ge(s_nmp, n - 1)
                V.tensor_reduce(nm[j % 2][:], S[j % 2][0:R, 0:HK].rearrange("q (h n) -> q h n", n=N),
                                AX_X, ALU.max, negate=True).then_inc(s_nm, 1)

            def evac_nmT(u, j):
                n = U * u + j
                dve.wait_ge(s_nmp, n + 1)
                if later(u) or j >= 2:
                    dve.wait_ge(s_sh, n - 1)
                V.tensor_copy(nmT[j % 2][:, 0:R], O[0:HEADS, NMT_COL:NMT_COL + 57].bitcast(BF16)[:, 0:R]).then_inc(s_nmT, 1)

            def normalise(u, b):
                dve.wait_ge(s_pv, U * u + 4 * b + 4)
                if later(u):
                    dve.wait_ge(s_on[b], u)
                o = O[0:R, 0:PAIRS * 4 * VC].rearrange("r (a f) -> r a f", f=VC)
                V.reciprocal(rec[b][:], o[:, :, 2 * D:VC]).then_inc(s_rec[b], 1)
                dve.wait_ge(s_rec[b], u + 1)
                if later(u):
                    dve.wait_ge(s_oTp[b], u)
                V.tensor_tensor(on[b][:].rearrange("r p (h e d) -> r (p h) e d", e=2, d=D),
                                o[:, :, 0:2 * D].rearrange("r a (e d) -> r a e d", d=D),
                                rec[b][:].unsqueeze(3).broadcast_to([R, 4 * PAIRS, 2, D]), ALU.mult).then_inc(s_on[b], 1)

            def add_attention(u, b):
                dve.wait_ge(s_pj[b], u + 1)
                dve.wait_ge(s_xres[b], u + 1)
                V.tensor_tensor(resid(u, b), M[2][0:R, 0:PAIRS * C].rearrange("r (p c) -> r p c", p=PAIRS), resid(u, b),
                                ALU.add).then_inc(s_x1[b], 1)

            def evac_zT(u, b):
                dve.wait_ge(s_zTp[b], u + 1)
                if later(u):
                    dve.wait_ge(s_f[b], 4 * u)
                V.tensor_scalar(zT[b][:].rearrange("c (p w n) -> c p w n", p=2, w=2),
                                M[3][:, 0:4 * W0].rearrange("c (p w n) -> c p w n", p=2, w=2)[:, :, :, 0:N],
                                n2w[:, 0:1], n2b[:, 0:1], ALU.mult, ALU.add).then_inc(s_zT[b], 1)

            def evac_m(u, b):
                dve.wait_ge(s_m[b], u + 1)
                if later(u):
                    dve.wait_ge(s_mo[b], u)
                V.tensor_scalar(mT[b][:, :, 0:N], M[3 - b][:, 0:T // 2].rearrange("c (w n) -> c w n", n=N),
                                fc2b[:, 0:1], None, ALU.add).then_inc(s_mT[b], 1)

            def result(u, b):
                dve.wait_ge(s_mo[b], u + 1)
                if later(u):
                    dve.wait_ge(s_out[b], 32 * u)
                V.tensor_tensor(res[b][:], M[3 - b][0:R, 0:PAIRS * C].rearrange("r (p c) -> r p c", p=PAIRS), resid(u, b),
                                ALU.add).then_inc(s_res[b], 1)

            def body(i):
                c, d, a = i - 1, i - 2, i + 1
                for k in range(U):
                    if k == 1 and on_chip(c):
                        dve.wait_ge(s_st2[0], 9 * c + 4)
                    if k == 5 and on_chip(c):
                        dve.wait_ge(s_st2[1], 9 * c + 4)
                    if on_chip(i):
                        neg_max(i, k)
                        evac_nmT(i, k)
                    if k == 0:
                        if on_chip(a):
                            ln1_stats(a, 0)
                            dve.wait_ge(s_st[0], 9 * a + 4)
                        if on_chip(c):
                            add_attention(c, 0)
                        if on_chip(a):
                            ln1_aggregate(a, 0)
                        if on_chip(c):
                            ln2_stats_ready(c, 0)
                        if on_chip(a):
                            ln1_eps(a, 0)
                        if on_chip(c):
                            ln2_stats(c, 0)
                    if k == 1:
                        if on_chip(c):
                            ln2_aggregate(c, 0)
                        if on_chip(d):
                            evac_m(d, 0)
                        if on_chip(i):
                            low_parts(i, 1)
                            repeat_parts(i, 1)
                    if k == 2:
                        if on_chip(d):
                            evac_m(d, 1)
                        if on_chip(c):
                            normalise(c, 1)
                        if on_chip(i):
                            place_k(i, 1)
                    if k == 3:
                        if on_chip(d):
                            result(d, 0)
                        if on_chip(i):
                            place_v(i, 1)
                        if on_chip(d):
                            result(d, 1)
                    if k == 4:
                        if on_chip(a):
                            ln1_stats(a, 1)
                            dve.wait_ge(s_st[1], 9 * a + 4)
                        if on_chip(c):
                            add_attention(c, 1)
                        if on_chip(a):
                            ln1_aggregate(a, 1)
                        if on_chip(c):
                            ln2_stats_ready(c, 1)
                        if on_chip(a):
                            ln1_eps(a, 1)
                        if on_chip(c):
                            ln2_stats(c, 1)
                            evac_zT(c, 0)
                    if k == 5:
                        if on_chip(c):
                            ln2_aggregate(c, 1)
                        if on_chip(a):
                            low_parts(a, 0)
                            repeat_parts(a, 0)
                    if k == 6:
                        if on_chip(i):
                            normalise(i, 0)
                        if on_chip(a):
                            place_k(a, 0)
                    if k == 7:
                        if on_chip(c):
                            evac_zT(c, 1)
                        if on_chip(a):
                            place_v(a, 0)

            rounds(dve, body)

        @block.tensor
        def _(pe):
            MM = nc.tensor.matmul
            pe.wait_ge(c_in, 16 * N_IN)
            pe.wait_ge(c_chain, C_TAB)
            MM(M[0][:, 0:TABLE], cpbw1[:], tab[:, 1, :], start=True, stop=True).then_inc(c_pe, 1)
            pe.wait_ge(c_chain, C_HID)
            for ch in range(2):
                rows = min(TCH, TABLE - ch * TCH)
                MM(M[1][0:rows, 8 * ch:8 * ch + HEADS], hidden[:, ch * TCH:ch * TCH + rows], cpbw2[:],
                   start=True, stop=True).then_inc(c_pe, 1)
            pe.wait_ge(c_chain, C_TBS)
            for key in range(N):
                for ch in range(2):
                    mm = MM(S[0][0:R, 0:HK].rearrange("q (h n) -> q h n", n=N)[:, :, key], onehot[:, ch, key, :], tbs[:, ch, :],
                            start=(ch == 0), stop=(ch == 1))
            mm.then_inc(c_pe, 1)
            pe.wait_ge(c_ready, 1)
            pe.wait_ge(c_zero, ZEROED)

            def scores(u, j):
                n, b, p = U * u + j, j // 4, j % 4
                if later(u) or j >= 2:
                    pe.wait_ge(s_e, n - 1)
                if p == 0:
                    pe.wait_ge(s_qx[b], u + 1)
                    pe.wait_ge(s_kx[b], 3 * (u + 1))
                    pe.wait_ge(s_kx3[b], u + 1)
                bank = S[j % 2]
                row = ((u % 4) // 3) if b == 1 else 0
                for part in range(3):
                    if isinstance(row, int):
                        src = biasp[:, (2 * row + (p == 3)) * 3 + part, :]
                    else:
                        src = biasp[:, bass.ds(row * 6 + (p == 3) * 3 + part, 1), :].rearrange("q o f -> q (o f)")
                    MM(bank[0:R, 0:HK], identb[0:R, 0:R], src, start=(part == 0), stop=False, skip_group_check=True)
                for w in range(2):
                    t = W0 * w
                    for g in range(2):
                        mm = MM(bank[W0 * w:W0 * w + N, 4 * N * g:4 * N * (g + 1)], qx[b][:, 4 * g + p, t:t + N],
                                kx[b][:, :, 4 * g + p, t:t + N], start=False, stop=False, skip_group_check=True)
                mm.then_inc(s_sc, 1)

            def turn_max(u, j):
                n = U * u + j
                pe.wait_ge(s_nm, n + 1)
                nc.tensor.transpose(O[0:HEADS, NMT_COL:NMT_COL + 57].bitcast(BF16)[:, 0:R], nm[j % 2][:],
                                    identb[0:R, 0:R]).then_inc(s_nmp, 1)

            def shift(u, j):
                n = U * u + j
                pe.wait_ge(s_nmT, n + 1)
                MM(S[j % 2][0:R, 0:HK], nmT[j % 2][:, 0:R], headsel[:], start=False, stop=True,
                   skip_group_check=True).then_inc(s_sh, 1)

            def turn_probs(u, j):
                n = U * u + j
                pe.wait_ge(s_e, n + 1)
                if later(u) or j >= 1:
                    pe.wait_ge(s_pT, n)
                src = probs[j % 2][:].rearrange("q h n -> q (h n)")
                for hp in range(4):
                    mm = nc.tensor.transpose(PT[0:R, R * hp:R * hp + R], src[:, 2 * W0 * hp:2 * W0 * hp + R],
                                             ident[0:R, 0:R])
                mm.then_inc(s_pTp, 1)

            def times_v(u, j):
                n, b, p = U * u + j, j // 4, j % 4
                pe.wait_ge(s_pT, n + 1)
                if p == 0:
                    pe.wait_ge(s_vx[b], 4 * u + 4)
                    if b == 1:
                        pe.wait_ge(s_on[0], u + 1)
                    elif later(u):
                        pe.wait_ge(s_on[1], u)
                for hp in range(4):
                    for w in range(2):
                        mm = MM(O[W0 * w:W0 * w + N, (4 * p + hp) * VC:(4 * p + hp + 1) * VC],
                                pT[j % 2][:, hp, W0 * w:W0 * w + N], vx[b][:, 2 * p + w, hp, :],
                                start=True, stop=True, tile_position=(0, W0 * w))
                mm.then_inc(s_pv, 1)

            def turn_tokens(dst, src, cols, sem_out):
                tokens = src[:].rearrange("r p c -> r (p c)")
                for pp in range(2):
                    mm = nc.tensor.transpose(dst[:, cols * pp:cols * pp + R], tokens[:, 2 * C * pp:2 * C * pp + 2 * C],
                                             ident[0:R, 0:R])
                mm.then_inc(sem_out, 1)

            def turn_y(u, b):
                pe.wait_ge(s_y1[b], u + 1)
                turn_tokens(M[0], y1[b], R, s_yTp[b])

            def turn_o(u, b):
                pe.wait_ge(s_on[b], u + 1)
                turn_tokens(M[1], on[b], R, s_oTp[b])

            def turn_z(u, b):
                pe.wait_ge(s_z1[b], u + 1)
                turn_tokens(M[3], z1[b], 2 * W0, s_zTp[b])

            def project_qkv(u, b, h):
                pe.wait_ge(s_yT[b], u + 1)
                rows = slice(C * h, C * h + C)
                for pp in range(2):
                    mm = MM(M[h][0:R, 3 * C * pp:3 * C * (pp + 1)], yT[b][rows, pp, 0:R], wqkv[rows, :],
                            start=True, stop=True)
                mm.then_inc(s_qkv[b], 1)

            def turn_qk(u, b, m):
                pe.wait_ge(s_dup[b], 3 * u + 3)
                dst = M[m][:, 0:4 * TP].bitcast(F16).rearrange("c (a n) -> c a n", n=TP)
                src = qkp[b][:].rearrange("r p h f -> r p (h f)")
                for g in range(2):
                    for p in range(PAIRS):
                        first = (2 * m + g) * 4 * HR
                        mm = nc.tensor.transpose(dst[:, 4 * g + p, 0:R], src[:, p, first:first + 4 * HR], identh[0:R, 0:R])
                mm.then_inc((s_qTp, s_kTp)[m][b], 1)

            def project_out(u, b):
                pe.wait_ge(s_oT[b], u + 1)
                for pp in range(2):
                    mm = MM(M[2][0:R, 2 * C * pp:2 * C * (pp + 1)], oT[b][:, pp, 0:R], wproj[:], start=True, stop=True)
                mm.then_inc(s_pj[b], 1)

            def fc1(u, b):
                pe.wait_ge(s_zT[b], u + 1)
                for n, (c, h) in enumerate(((0, 0), (1, 1), (0, 1), (1, 0))):
                    if n >= 2:
                        pe.wait_ge(s_f[b], 4 * u + n - 1)
                    rows = slice(C * h, C * h + C)
                    MM(M[FC_BANK[b] + c][:, h * T // 2:(h + 1) * T // 2], w1[rows, 128 * c:128 * c + 128], zT[b][rows, :],
                       start=True, stop=True).then_inc(s_f[b], 1)

            def fc2(u, b):
                pe.wait_ge(s_g[b], 2 * u + 2)
                for h in range(2):
                    for c in range(2):
                        mm = MM(M[3 - b][C * h:C * h + C, 0:T // 2], w2[:, c, :], gl[b][:, c, h * T // 2:(h + 1) * T // 2],
                                start=(c == 0), stop=(c == 1), tile_position=(0, C * h))
                mm.then_inc(s_m[b], 1)

            def turn_back(u, b):
                pe.wait_ge(s_mT[b], u + 1)
                src = mT[b][:].rearrange("c w n -> c (w n)")
                for pp in range(2):
                    mm = nc.tensor.transpose(M[3 - b][0:R, 2 * C * pp:2 * C * pp + 2 * C], src[:, 2 * W0 * pp:2 * W0 * pp + R],
                                             ident[:])
                mm.then_inc(s_mo[b], 1)

            def after(*uses):
                for u, semaphore, count in uses:
                    if on_chip(u):
                        pe.wait_ge(semaphore, count)
                        return

            def body(i):
                c, d = i - 1, i - 2
                a = i + 1
                y = [(a, s_yT[b], a + 1) for b in range(2)]
                o_c1, o_i0 = (c, s_oT[1], c + 1), (i, s_oT[0], i + 1)
                proj = [(c, s_x1[b], c + 1) for b in range(2)]
                z = [(c, s_zT[b], c + 1) for b in range(2)]
                q_i1, k_i1 = (i, s_qx[1], i + 1), (i, s_kx[1], 3 * i + 3)
                q_a0, k_a0 = (a, s_qx[0], a + 1), (a, s_kx[0], 3 * a + 3)
                back = [(d, s_res[b], d + 1) for b in range(2)]
                k3_i1, k3_a0 = (i, s_kx3[1], i + 1), (a, s_kx3[0], a + 1)
                gelu_d1 = (d, s_g[1], 2 * d + 2)
                gelu_d0 = (d, s_g[0], 2 * d + 2)
                for k in range(U):
                    u1, j1 = at_unit(i, k, 1)
                    if on_chip(u1):
                        shift(u1, j1)
                    if on_chip(i):
                        scores(i, k)
                    u3, j3 = at_unit(i, k, 3)
                    if on_chip(u3):
                        times_v(u3, j3)
                    u2, j2 = at_unit(i, k, 2)
                    if on_chip(u2):
                        turn_probs(u2, j2)
                    if on_chip(i):
                        turn_max(i, k)
                    if k == 0:
                        if on_chip(c):
                            after(gelu_d0)
                            project_out(c, 0)
                        if on_chip(d):
                            fc2(d, 0)
                        if on_chip(i):
                            after(gelu_d1)
                            project_qkv(i, 1, 0)
                            project_qkv(i, 1, 1)
                    if k == 1:
                        if on_chip(d):
                            after(proj[0])
                            fc2(d, 1)
                    if k == 2:
                        if on_chip(i):
                            turn_qk(i, 1, 0)
                            turn_qk(i, 1, 1)
                        if on_chip(d):
                            turn_back(d, 0)
                    if k == 3:
                        if on_chip(d):
                            turn_back(d, 1)
                        if on_chip(c):
                            after(k_i1, gelu_d1)
                            after(k3_i1)
                            turn_o(c, 1)
                        if on_chip(a):
                            after(q_i1)
                            turn_y(a, 0)
                    if k == 4:
                        if on_chip(c):
                            after(back[1], proj[0])
                            project_out(c, 1)
                            after(back[0])
                            turn_z(c, 0)
                        if on_chip(a):
                            project_qkv(a, 0, 0)
                            after(o_c1, k_i1)
                            if not on_chip(c):
                                after(k3_i1)
                            project_qkv(a, 0, 1)
                    if k == 6:
                        if on_chip(a):
                            turn_qk(a, 0, 0)
                            turn_qk(a, 0, 1)
                    if k == 7:
                        if on_chip(c):
                            after(z[0])
                            turn_z(c, 1)
                        if on_chip(a):
                            after(q_a0)
                            turn_y(a, 1)
                        if on_chip(i):
                            after(k_a0, o_c1)
                            after(k3_a0)
                            turn_o(i, 0)
                        if on_chip(c):
                            after(proj[1])
                            pe.wait_ge(s_zT[1], c + 1)
                            fc1(c, 0)
                            after(y[1], q_i1, gelu_d1)
                            after(o_i0, o_c1)
                            fc1(c, 1)

            rounds(pe, body)


FC_BANK = (2, 0)


def shape_constants():
    ident = np.eye(128, dtype=np.float32)
    co = np.stack(np.meshgrid(np.arange(WIN), np.arange(WIN), indexing="ij")).reshape(2, -1)
    rel = co[:, :, None] - co[:, None, :]
    idx = (rel[0] + WIN - 1) * (2 * WIN - 1) + rel[1] + WIN - 1
    onehot = np.zeros((2 * TCH, N, R), np.float32)
    for q in range(N):
        for k in range(N):
            for w in range(2):
                onehot[idx[q, k], k, W0 * w + q] = 1.0
    onehot = np.ascontiguousarray(onehot.reshape(2, TCH, N, R))
    mask = np.zeros((R, 4, N), np.float32)
    part = np.where(np.arange(WIN) < WIN - SHIFT, 0, 1)
    for v in range(4):
        for w in range(2):
            rows = part[co[0]] * (v // 2)
            cols = part[co[1]] * (1 if v % 2 and w == 1 else 0)
            region = 2 * rows + cols
            mask[W0 * w:W0 * w + N, v] = np.where(region[:, None] != region[None, :], -1e9, 0.0)
    line = (np.arange(-(WIN - 1), WIN, dtype=np.float32) / np.float32(WIN - 1)).astype(np.float32)
    grid = np.stack(np.meshgrid(line, line, indexing="ij")).reshape(2, -1).astype(np.float32)
    headsel = np.zeros((HEADS, HEADS, N), np.float32)
    for h in range(HEADS):
        headsel[h, h] = 1.0
    return ident, onehot, mask, np.ascontiguousarray(grid), headsel.reshape(HEADS, HK)


def kernel(x, L0_conv_norm1_w, L0_conv_norm1_b, L0_conv_qkv_w, L0_conv_proj_w, L0_conv_proj_b, L0_conv_cpb_w1,
           L0_conv_cpb_b1, L0_conv_cpb_w2, L0_conv_h_times, L0_conv_pow_para, L0_conv_ws_scalar, L0_conv_ws_scalar2,
           L0_conv_norm2_w, L0_conv_norm2_b, L0_conv_fc1_w, L0_conv_fc1_b, L0_conv_fc2_w, L0_conv_fc2_b):
    import concourse.bacc as bacc
    from concourse.bass_utils import run_bass_kernel_spmd

    B, H, W, _ = x.shape
    nh, nw = H // WIN, W // WIN

    def rows(a):
        return np.broadcast_to(np.asarray(a).reshape(1, -1), (R, np.asarray(a).size))

    xs = np.roll(np.asarray(x), (-SHIFT, -SHIFT), axis=(1, 2))
    xs = xs.reshape(B, nh, WIN, PAIRS, 2, WIN, C).transpose(0, 1, 4, 2, 5, 3, 6).reshape(B * nh, 2, N, PAIRS, C)
    ident, onehot, mask, grid, headsel = shape_constants()
    twice = lambda a: np.tile(np.asarray(a).reshape(C, 1), (2, 1))
    two = lambda a: np.broadcast_to(np.asarray(a).reshape(1, 1), (2, 1))
    fc2_wT = np.asarray(L0_conv_fc2_w).T.reshape(2, 128, C).transpose(1, 0, 2)
    ins = {
        "x": xs, "norm1_w": twice(L0_conv_norm1_w), "norm1_b": twice(L0_conv_norm1_b),
        "qkv_wT": np.asarray(L0_conv_qkv_w).T, "proj_wT": np.asarray(L0_conv_proj_w).T, "proj_b": rows(L0_conv_proj_b),
        "cpb_w1T": np.asarray(L0_conv_cpb_w1).T, "cpb_b1": np.asarray(L0_conv_cpb_b1).reshape(-1, 1),
        "cpb_w2T": np.asarray(L0_conv_cpb_w2).T, "h_times": two(L0_conv_h_times), "pow_para": two(L0_conv_pow_para),
        "ws_scalar": two(L0_conv_ws_scalar), "ws_scalar2": two(L0_conv_ws_scalar2),
        "norm2_w": twice(L0_conv_norm2_w), "norm2_b": twice(L0_conv_norm2_b), "fc1_wT": np.asarray(L0_conv_fc1_w).T,
        "fc1_b": np.asarray(L0_conv_fc1_b).reshape(2, 128).T, "fc2_wT": fc2_wT, "fc2_b": twice(L0_conv_fc2_b),
        "c_ident": ident, "c_onehot": onehot, "c_mask": mask, "c_grid": grid, "c_headsel": headsel,
    }
    nc = bacc.Bacc("TRN2", target_bir_lowering=False, num_devices=1)
    arrays, aps = {}, {}
    for name, a in ins.items():
        a = np.ascontiguousarray(a)
        arrays["in_" + name] = a
        aps[name] = nc.dram_tensor("in_" + name, a.shape, mybir.dt.from_np(a.dtype), kind="ExternalInput").ap()
    out = nc.dram_tensor("out", xs.shape, F32, kind="ExternalOutput").ap()
    swin_block(nc, out=out, **aps)
    r = run_bass_kernel_spmd(nc, [arrays], core_ids=[0])
    got = r.results[0]["out"]
    got = got.reshape(B, nh, 2, WIN, WIN, PAIRS, C).transpose(0, 1, 3, 5, 2, 4, 6).reshape(B, H, W, C)
    return np.roll(got, (SHIFT, SHIFT), axis=(1, 2))
```

```python
from contextlib import ExitStack

import numpy as np

import concourse.bass as bass
from concourse import mybir

F32 = mybir.dt.float32
F16 = mybir.dt.float16
ACT = mybir.ActivationFunctionType
ALU = mybir.AluOpType
AX_X = mybir.AxisListType.X

WIN = 7
N = WIN * WIN
SHIFT = 3
HEADS = 8
D = 8
C = HEADS * D
HID = 4 * C
PAIRS = 4
W0 = 64
R = W0 + N
T = PAIRS * 2 * N
HK = HEADS * N
QKH = 2 * HEADS
HR = 32
TP = R + 1
TABLE = (2 * WIN - 1) ** 2
TCH = (TABLE + 1) // 2
R0 = 96
VC = 2 * D + 2
EPS = 1e-5
ZSCALE = 64.0
U = 8
FC_BANK = (2, 0)
FC_ORDER = ((0, 1), (1, 0))
XRING = 4


def swin_block(nc, x, norm1_w, norm1_b, qkv_wT, proj_wT, proj_b, cpb_w1T, cpb_b1, cpb_w2T, h_times,
               pow_para, ws_scalar, ws_scalar2, norm2_w, norm2_b, fc1_wT, fc1_b, fc2_wT, fc2_b,
               c_ident, c_onehot, c_left, c_right, c_grid, c_headsel, out):
    NB = x.shape[0]
    NSB = NB // 2
    ctx = ExitStack()
    with ctx:
        def sb(name, shape, dt=F32):
            return ctx.enter_context(nc.sbuf_tensor(name, shape, dt))

        def ps(name):
            return ctx.enter_context(nc.psum_tensor(name, [128, 512], F32))

        def sem(name):
            return ctx.enter_context(nc.semaphore(name))

        ident = sb("ident", [128, 128])
        identh = sb("identh", [128, 128], F16)
        onehot = sb("onehot", [TCH, 2, N, R])
        grid = sb("grid", [2, TABLE])
        n1w, n1b, n2w, n2b, fc2b = (sb(name, [2 * C, 1]) for name in ("n1w", "n1b", "n2w", "n2b", "fc2b"))
        projb = sb("projb", [R, C])
        wqkv = sb("wqkv", [2 * C, 3 * C])
        wproj = sb("wproj", [2 * C, 2 * C])
        w1 = sb("w1", [2 * C, HID])
        w1s = sb("w1s", [2 * C, HID])
        w1p = sb("w1p", [2 * C, 2, HID], F16)
        b1z = sb("b1z", [2 * C, 2])
        w2 = sb("w2", [128, 2, C])
        b1 = sb("b1", [128, 2])
        cpbw1 = sb("cpbw1", [2, 128])
        cpbb1 = sb("cpbb1", [128, 1])
        cpbw2 = sb("cpbw2", [128, HEADS])
        scal = sb("scal", [2, 4])
        st = sb("st", [2, 12, 4])
        tab = sb("tab", [2, 6, TABLE])
        hidden = sb("hidden", [128, 2 * TCH])
        tbs = sb("tbs", [TCH, 2, HEADS])
        mhalf = sb("mhalf", [R, PAIRS])
        bias_t = sb("bias_t", [R, HK])
        left = sb("left", [128, TP], F16)
        bias_hi = sb("bias_hi", [128, 4, HK], F16)
        bias_lo = sb("bias_lo", [128, HK], F16)

        xin = [sb(f"xin{b}", [R, PAIRS, C]) for b in range(2)]
        xres = sb("xres", [R, XRING * 2, PAIRS * C])
        stats = [sb(f"stats{b}", [R, PAIRS, 6]) for b in range(2)]
        mv = [sb(f"mv{b}", [R, PAIRS, 2]) for b in range(2)]
        veps = [sb(f"veps{b}", [R, PAIRS]) for b in range(2)]
        rstd = [sb(f"rstd{b}", [R, PAIRS]) for b in range(2)]
        y0 = [sb(f"y0{b}", [R, PAIRS, C]) for b in range(2)]
        y1 = [sb(f"y1{b}", [R, PAIRS, C]) for b in range(2)]
        yT = [sb(f"yT{b}", [2 * C, 2, 128]) for b in range(2)]
        qkp = [sb(f"qkp{b}", [R, PAIRS, QKH, HR], F16) for b in range(2)]
        vs = [sb(f"vs{b}", [R, PAIRS, C]) for b in range(2)]
        qx = [sb(f"qx{b}", [128, 2 * PAIRS, 2, N], F16) for b in range(2)]
        kx = [sb(f"kx{b}", [128, 4, 2 * PAIRS, 2, N], F16) for b in range(2)]
        vx = [sb(f"vx{b}", [R, 2 * PAIRS, 4, VC]) for b in range(2)]
        nm = [sb(f"nm{n}", [R, 128 - R0], F16) for n in range(2)]
        nmT = [sb(f"nmT{n}", [128, TP], F16) for n in range(2)]
        probs = [sb(f"probs{n}", [R, HEADS, W0]) for n in range(2)]
        pT = [sb(f"pT{n}", [R, 4, R]) for n in range(2)]
        rec = [sb(f"rec{b}", [R, 4 * PAIRS, 2]) for b in range(2)]
        on = [sb(f"on{b}", [R, PAIRS, C]) for b in range(2)]
        oT = [sb(f"oT{b}", [2 * C, 2, 128]) for b in range(2)]
        stats2 = [sb(f"stats2{b}", [R, PAIRS, 6]) for b in range(2)]
        mv2 = [sb(f"mv2{b}", [R, PAIRS, 2]) for b in range(2)]
        veps2 = [sb(f"veps2{b}", [R, PAIRS]) for b in range(2)]
        rstd2 = [sb(f"rstd2{b}", [R, PAIRS]) for b in range(2)]
        z0 = [sb(f"z0{b}", [R, PAIRS, C]) for b in range(2)]
        z1 = [sb(f"z1{b}", [R, PAIRS, C]) for b in range(2)]
        zp = [sb(f"zp{b}", [R, PAIRS, 2, C], F16) for b in range(2)]
        zT = [sb(f"zT{b}", [2 * C, T], F16) for b in range(2)]
        gl = [sb(f"gl{b}", [128, 2, T]) for b in range(2)]
        mT = [sb(f"mT{b}", [2 * C, PAIRS, W0]) for b in range(2)]
        res = [sb(f"res{b}", [R, PAIRS, C]) for b in range(2)]

        S = [ps(f"S{n}") for n in range(2)]
        PT = ps("PT")
        O = ps("O")
        M = [ps(f"M{n}") for n in range(4)]
        NMT_COL = PAIRS * 4 * VC

        c_in = sem("c_in")
        c_zero = sem("c_zero")
        c_chain = sem("c_chain")
        c_ready = sem("c_ready")
        c_bias = sem("c_bias")
        c_spread = sem("c_spread")
        c_act = sem("c_act")
        c_pool = sem("c_pool")
        c_pe = sem("c_pe")
        s_x = [sem(f"s_x{b}") for b in range(2)]
        s_st = [sem(f"s_st{b}") for b in range(2)]
        s_rs = [sem(f"s_rs{b}") for b in range(2)]
        s_y0 = [sem(f"s_y0{b}") for b in range(2)]
        s_y1 = [sem(f"s_y1{b}") for b in range(2)]
        s_xres = [sem(f"s_xres{b}") for b in range(2)]
        s_yTp = [sem(f"s_yTp{b}") for b in range(2)]
        s_yT = [sem(f"s_yT{b}") for b in range(2)]
        s_qkv = [sem(f"s_qkv{b}") for b in range(2)]
        s_vs = [sem(f"s_vs{b}") for b in range(2)]
        s_lo = [sem(f"s_lo{b}") for b in range(2)]
        s_dup = [sem(f"s_dup{b}") for b in range(2)]
        s_qTp = [sem(f"s_qTp{b}") for b in range(2)]
        s_kTp = [sem(f"s_kTp{b}") for b in range(2)]
        s_qx = [sem(f"s_qx{b}") for b in range(2)]
        s_kx = [sem(f"s_kx{b}") for b in range(2)]
        s_kx3 = [sem(f"s_kx3{b}") for b in range(2)]
        s_vx = [sem(f"s_vx{b}") for b in range(2)]
        s_sc = sem("s_sc")
        s_nm = sem("s_nm")
        s_nmp = sem("s_nmp")
        s_nmT = sem("s_nmT")
        s_sh = sem("s_sh")
        s_e = sem("s_e")
        s_pTp = sem("s_pTp")
        s_pT = sem("s_pT")
        s_pv = sem("s_pv")
        s_rec = [sem(f"s_rec{b}") for b in range(2)]
        s_on = [sem(f"s_on{b}") for b in range(2)]
        s_oTp = [sem(f"s_oTp{b}") for b in range(2)]
        s_oT = [sem(f"s_oT{b}") for b in range(2)]
        s_pj = [sem(f"s_pj{b}") for b in range(2)]
        s_x1 = [sem(f"s_x1{b}") for b in range(2)]
        s_st2 = [sem(f"s_st2{b}") for b in range(2)]
        s_rs2 = [sem(f"s_rs2{b}") for b in range(2)]
        s_z0 = [sem(f"s_z0{b}") for b in range(2)]
        s_z1 = [sem(f"s_z1{b}") for b in range(2)]
        s_zp = [sem(f"s_zp{b}") for b in range(2)]
        s_zTp = [sem(f"s_zTp{b}") for b in range(2)]
        s_zT = [sem(f"s_zT{b}") for b in range(2)]
        s_f = [sem(f"s_f{b}") for b in range(2)]
        s_g = [sem(f"s_g{b}") for b in range(2)]
        s_m = [sem(f"s_m{b}") for b in range(2)]
        s_mT = [sem(f"s_mT{b}") for b in range(2)]
        s_mo = [sem(f"s_mo{b}") for b in range(2)]
        s_res = [sem(f"s_res{b}") for b in range(2)]
        s_out = [sem(f"s_out{b}") for b in range(2)]

        N_IN = 26
        ZEROED = 16
        C_ABS, C_POW, C_TAB, C_HID, C_TBS = 3, 13, 18, 19, 22

        def on_chip(u):
            return not isinstance(u, int) or 0 <= u < NSB

        def later(u, k=1):
            return not isinstance(u, int) or u >= k

        def rounds(eng, body):
            for i in range(-1, 3):
                body(i)
            pairs = (NSB - 5) // 2
            with eng.Fori(3, 3 + 2 * pairs, 2) as i:
                body(i)
                body(i + 1)
            for i in range(3 + 2 * pairs, NSB + 2):
                body(i)

        def at_unit(i, k, back):
            return i + (k - back) // U, (k - back) % U

        def tokens16(bank, rows):
            return bank[rows, :].bitcast(F16).rearrange("c (a w n) -> c a w n", w=2, n=W0)[:, :, :, 0:N]

        def resid(u, b):
            return xres[:, bass.ds((u % XRING) * 2 + b, 1), :].rearrange("r o (p c) -> r (o p) c", p=PAIRS)

        block = ctx.enter_context(nc.Block())

        @block.sync
        def _(sp):
            ins = [(ident[:], c_ident), (onehot[:, 0], c_onehot[0]), (onehot[:, 1], c_onehot[1]),
                   (left[:], c_left), (grid[:], c_grid),
                   (n1w[:], norm1_w), (n1b[:], norm1_b), (n2w[:], norm2_w), (n2b[:], norm2_b),
                   (projb[:], proj_b), (fc2b[:], fc2_b), (wqkv[0:C], qkv_wT), (wqkv[C:2 * C], qkv_wT), (w1[0:C], fc1_wT),
                   (w1[C:2 * C], fc1_wT),
                   (w2[:], fc2_wT), (b1[:], fc1_b), (cpbw1[:], cpb_w1T), (cpbb1[:], cpb_b1),
                   (cpbw2[:], cpb_w2T), (scal[:, 0:1], h_times), (scal[:, 1:2], ws_scalar),
                   (scal[:, 2:3], ws_scalar2), (scal[:, 3:4], pow_para)]
            for dst, src in ins:
                sp.dma_start(dst, src).then_inc(c_in, 16)
            sp.wait_ge(c_zero, 1)
            for h in range(2):
                sp.dma_start(wproj[C * h:C * h + C, C * h:C * h + C], proj_wT).then_inc(c_in, 16)
            sp.wait_ge(c_zero, ZEROED)

            sp.wait_ge(c_bias, 1)
            for v in range(4):
                sp.dma_start(bias_hi[N:N + 8, v, :], c_right[v, 0]).then_inc(c_spread, 16)
                sp.dma_start(bias_hi[R:R + 8, v, :], c_right[v, 1]).then_inc(c_spread, 16)
            sp.dma_start(bias_lo[R:R + HEADS, :], c_headsel).then_inc(c_spread, 16)

            def load(u, b):
                src = [x[2 * u + b, w] for w in range(2)]
                if later(u):
                    sp.wait_ge(s_y0[b], u)
                    sp.wait_ge(s_xres[b], u)
                for w in range(2):
                    sp.dma_start(xin[b][W0 * w:W0 * w + N], src[w]).then_inc(s_x[b], 16)

            def store(u, b):
                sp.wait_ge(s_res[b], u + 1)
                for w in range(2):
                    sp.dma_start(out[2 * u + b, w], res[b][W0 * w:W0 * w + N]).then_inc(s_out[b], 16)

            load(0, 0)
            load(0, 1)

            def body(i):
                if on_chip(i + 2):
                    load(i + 2, 0)
                if on_chip(i - 2):
                    store(i - 2, 0)
                    store(i - 2, 1)
                if on_chip(i + 2):
                    load(i + 2, 1)

            rounds(sp, body)
            for b in range(2):
                sp.wait_ge(s_out[b], 32 * NSB)

        @block.gpsimd
        def _(pool):
            nc.gpsimd.memset(wproj[:], 0.0).then_inc(c_zero, 1)
            for b in range(2):
                nc.gpsimd.memset(xin[b][:], 0.0).then_inc(c_zero, 1)
                nc.gpsimd.memset(kx[b][:], 0.0).then_inc(c_zero, 1)
                nc.gpsimd.memset(mT[b][:], 0.0).then_inc(c_zero, 1)
                nc.gpsimd.memset(probs[b][:], 0.0).then_inc(c_zero, 1)
                nc.gpsimd.memset(nmT[b][:], 0.0).then_inc(c_zero, 1)
                nc.gpsimd.memset(nm[b][:], 0.0).then_inc(c_zero, 1)
            nc.gpsimd.memset(bias_hi[:], 0.0).then_inc(c_zero, 1)
            nc.gpsimd.memset(bias_lo[:], 0.0).then_inc(c_zero, 1)
            nc.gpsimd.memset(mhalf[:], -0.5).then_inc(c_zero, 1)
            pool.wait_ge(c_zero, ZEROED)
            pool.wait_ge(c_chain, C_POW)
            nc.gpsimd.tensor_tensor(tab[:, 4, :], tab[:, 3, :], tab[:, 5, :], ALU.pow).then_inc(c_pool, 1)

            def ln_rstd(veps_b, rstd_b, s_veps, s_rs_b, u, s_used):
                pool.wait_ge(s_veps, 9 * u + 9)
                if later(u):
                    pool.wait_ge(s_used, u)
                nc.gpsimd.tensor_tensor(rstd_b[:], veps_b[:], mhalf[:], ALU.pow).then_inc(s_rs_b, 1)

            def normalise_rows(src, mv_b, rstd_b, a0, a1, s_rs_b, s0, s1, s_used, u):
                pool.wait_ge(s_rs_b, u + 1)
                if later(u):
                    pool.wait_ge(s1, u)
                nc.gpsimd.tensor_tensor(a0[:], src, mv_b[:, :, 0:1].broadcast_to([R, PAIRS, C]), ALU.subtract).then_inc(s0, 1)
                pool.wait_ge(s0, u + 1)
                if later(u):
                    pool.wait_ge(s_used, u)
                nc.gpsimd.tensor_tensor(a1[:], a0[:], rstd_b[:].unsqueeze(2).broadcast_to([R, PAIRS, C]),
                                        ALU.mult).then_inc(s1, 1)

            def keep_residual(u, b):
                if later(u, XRING):
                    pool.wait_ge(s_res[b], u - XRING + 1)
                pool.wait_ge(s_x[b], 32 * u + 32)
                nc.gpsimd.tensor_tensor(resid(u, b), xin[b][:], projb[:].unsqueeze(1).broadcast_to([R, PAIRS, C]),
                                        ALU.add).then_inc(s_xres[b], 1)

            def ln1_rstd(u, b):
                ln_rstd(veps[b], rstd[b], s_st[b], s_rs[b], u, s_y1[b])

            def ln2_rstd(u, b):
                ln_rstd(veps2[b], rstd2[b], s_st2[b], s_rs2[b], u, s_z1[b])

            def ln1_rows(u, b):
                normalise_rows(xin[b][:], mv[b], rstd[b], y0[b], y1[b], s_rs[b], s_y0[b], s_y1[b], s_yTp[b], u)

            def ln2_rows(u, b):
                rstd_b = rstd2[b][:].unsqueeze(2).broadcast_to([R, PAIRS, C])
                pool.wait_ge(s_rs2[b], u + 1)
                if later(u):
                    pool.wait_ge(s_zp[b], 2 * u)
                nc.gpsimd.tensor_tensor(z0[b][:], resid(u, b), mv2[b][:, :, 0:1].broadcast_to([R, PAIRS, C]),
                                        ALU.subtract).then_inc(s_z0[b], 1)
                pool.wait_ge(s_z0[b], u + 1)
                nc.gpsimd.tensor_tensor(z1[b][:], z0[b][:], rstd_b, ALU.mult).then_inc(s_z1[b], 1)
                if later(u):
                    pool.wait_ge(s_zTp[b], u)
                nc.gpsimd.tensor_tensor(zp[b][:, :, 0, :], z0[b][:], rstd_b, ALU.mult).then_inc(s_zp[b], 1)
                pool.wait_ge(s_zp[b], 2 * u + 1)
                pool.wait_ge(s_z1[b], u + 1)
                nc.gpsimd.tensor_tensor(zp[b][:, :, 1, :], z1[b][:], zp[b][:, :, 0, :], ALU.subtract).then_inc(s_zp[b], 1)

            def body(i):
                c, a = i - 1, i + 1
                if on_chip(c):
                    ln2_rstd(c, 0)
                if on_chip(a):
                    ln1_rstd(a, 0)
                    ln1_rows(a, 0)
                if on_chip(c):
                    ln2_rows(c, 0)
                if on_chip(a):
                    keep_residual(a, 0)
                if on_chip(a):
                    ln1_rstd(a, 1)
                    ln1_rows(a, 1)
                if on_chip(c):
                    ln2_rstd(c, 1)
                    ln2_rows(c, 1)
                if on_chip(a):
                    keep_residual(a, 1)

            rounds(pool, body)

        @block.scalar
        def _(act):
            act.wait_ge(c_chain, C_ABS)
            nc.scalar.activation(st[:, 2, 0:3], st[:, 1, 0:3], ACT.Exp, scale=-1.0).then_inc(c_act, 1)
            nc.scalar.activation(st[:, 3, 0:1], scal[:, 3:4], ACT.Exp, scale=-1.0).then_inc(c_act, 1)
            act.wait_ge(c_act, 2)
            nc.scalar.activation(st[:, 4, 0:3], st[:, 2, 0:3], ACT.Ln, bias=1.0).then_inc(c_act, 1)

            def evac_yT(u, b):
                act.wait_ge(s_yTp[b], u + 1)
                if later(u):
                    act.wait_ge(s_qkv[b], 2 * u)
                nc.scalar.activation(yT[b][:, :, 0:R], M[0][:, 0:2 * R].rearrange("c (p r) -> c p r", p=2),
                                     ACT.Identity, bias=n1b[:, 0:1], scale=n1w[:, 0:1]).then_inc(s_yT[b], 1)

            def evac_m(u, b):
                act.wait_ge(s_m[b], u + 1)
                if later(u):
                    act.wait_ge(s_mo[b], u)
                nc.scalar.activation(mT[b][:, :, 0:N], M[3 - b][:, 0:T // 2].rearrange("c (w n) -> c w n", n=N),
                                     ACT.Identity, bias=fc2b[:, 0:1]).then_inc(s_mT[b], 1)

            def evac_zT(u):
                act.wait_ge(s_zTp[0], u + 1)
                if later(u):
                    act.wait_ge(s_f[0], 2 * u)
                nc.scalar.activation(zT[0][:].rearrange("c (w n) -> c w n", n=N),
                                     M[3][:, 0:4 * W0].bitcast(F16).rearrange("c (w n) -> c w n", n=W0)[:, :, 0:N],
                                     ACT.Copy).then_inc(s_zT[0], 1)

            def evac_oT(u, b):
                act.wait_ge(s_oTp[b], u + 1)
                if later(u):
                    act.wait_ge(s_pj[b], u)
                nc.scalar.activation(oT[b][:, :, 0:R], M[0][:, 2 * R:4 * R].rearrange("c (p r) -> c p r", p=2),
                                     ACT.Copy).then_inc(s_oT[b], 1)

            def keep_qkv(u, b):
                for h in range(2):
                    bank = M[h][0:R, 0:2 * 3 * C].rearrange("r (p f) -> r p f", p=2)
                    act.wait_ge(s_qkv[b], 2 * u + h + 1)
                    if later(u):
                        act.wait_ge(s_kTp[b], u)
                        act.wait_ge(s_vx[b], 4 * u)
                    nc.scalar.activation(qkp[b][:, h::2, :, 0:D],
                                         bank[:, :, 0:2 * C].rearrange("r p (h d) -> r p h d", d=D),
                                         ACT.Copy)
                    nc.scalar.activation(vs[b][:, h::2, :], bank[:, :, 2 * C:3 * C], ACT.Copy).then_inc(s_vs[b], 1)

            def place_qk(u, b):
                act.wait_ge(s_qTp[b], u + 1)
                if later(u):
                    act.wait_ge(s_sc, U * (u - 1) + 4 * b + 4)
                nc.scalar.activation(qx[b][:], tokens16(M[0], slice(0, 128)),
                                     ACT.Copy).then_inc(s_qx[b], 1)
                act.wait_ge(s_kTp[b], u + 1)
                for h in (2, 3):
                    rows = slice(HR * h, HR * h + HR)
                    nc.scalar.activation(kx[b][rows, h], tokens16(M[1], rows),
                                         ACT.Copy).then_inc(s_kx3[b], 1)

            def exp(u, j):
                n = U * u + j
                act.wait_ge(s_sh, n + 1)
                if later(u) or j >= 2:
                    act.wait_ge(s_pTp, n - 1)
                nc.scalar.activation(probs[j % 2][:, :, 0:N], S[j % 2][0:R, 0:HK].rearrange("q (h n) -> q h n", n=N),
                                     ACT.Exp).then_inc(s_e, 1)

            def evac_pT(u, j):
                n = U * u + j
                act.wait_ge(s_pTp, n + 1)
                if later(u) or j >= 2:
                    act.wait_ge(s_pv, n - 1)
                nc.scalar.activation(pT[j % 2][:].rearrange("k h r -> k (h r)"), PT[0:R, 0:4 * R],
                                     ACT.Copy).then_inc(s_pT, 1)

            def gelu(u, b):
                for n, c in enumerate(FC_ORDER[b]):
                    act.wait_ge(s_f[b], 2 * u + 1 + n)
                    if later(u):
                        act.wait_ge(s_m[b], u)
                    nc.scalar.activation(gl[b][:, c, :], M[FC_BANK[b] + c][:, 0:T], ACT.Gelu,
                                         bias=b1z[:, c:c + 1], scale=ZSCALE ** -2.0).then_inc(s_g[b], 1)

            def body(i):
                c, d, a = i - 1, i - 2, i + 1
                for k in range(U):
                    u, j = at_unit(i, k, 1)
                    if on_chip(u):
                        exp(u, j)
                    u, j = at_unit(i, k, 2)
                    if on_chip(u):
                        evac_pT(u, j)
                    if k == 0 and on_chip(i):
                        keep_qkv(i, 1)
                    if k == 1 and on_chip(d):
                        evac_m(d, 0)
                        evac_m(d, 1)
                    if k == 2 and on_chip(i):
                        place_qk(i, 1)
                    if k == 5 and on_chip(c):
                        evac_zT(c)
                    if k == 3:
                        if on_chip(c):
                            evac_oT(c, 1)
                        if on_chip(a):
                            evac_yT(a, 0)
                    if k == 4 and on_chip(a):
                        keep_qkv(a, 0)
                    if k == 6 and on_chip(a):
                        place_qk(a, 0)
                    if k == 7:
                        if on_chip(c):
                            gelu(c, 0)
                            gelu(c, 1)

            rounds(act, body)

        @block.vector
        def _(dve):
            steps = [0]

            def then(ins):
                steps[0] += 1
                ins.then_inc(c_chain, 1)
                dve.wait_ge(c_chain, steps[0])

            V = nc.vector
            dve.wait_ge(c_in, 16 * N_IN)
            then(V.tensor_scalar(st[:, 0, 0:3], scal[:, 0:3], -1.0, None, ALU.mult))
            then(V.tensor_tensor(st[:, 1, 0:3], scal[:, 0:3], st[:, 0, 0:3], ALU.max))
            then(V.tensor_scalar(st[:, 5, 0:3], scal[:, 0:3], 0.0, None, ALU.max))
            dve.wait_ge(c_act, 3)
            then(V.tensor_tensor(st[:, 6, 0:3], st[:, 5, 0:3], st[:, 4, 0:3], ALU.add))
            then(V.tensor_scalar(st[:, 7, 0:1], st[:, 3, 0:1], 1.0, None, ALU.add))
            then(V.reciprocal(st[:, 8, 0:1], st[:, 7, 0:1]))
            then(V.reciprocal(st[:, 9, 0:1], st[:, 6, 2:3]))
            then(V.tensor_scalar(tab[:, 0, :], grid[:], st[:, 6, 0:1], None, ALU.mult))
            then(V.tensor_scalar(tab[:, 1, :], tab[:, 0, :], -1.0, None, ALU.mult))
            then(V.tensor_tensor(tab[:, 2, :], tab[:, 0, :], tab[:, 1, :], ALU.max))
            then(V.tensor_scalar(tab[:, 3, :], tab[:, 2, :], st[:, 6, 1:2], 1e-6, ALU.mult, ALU.add))
            then(V.tensor_scalar(tab[:, 1, :], tab[:, 0, :], 0.0, None, ALU.mult))
            then(V.tensor_scalar(tab[:, 5, :], tab[:, 1, :], st[:, 8, 0:1], None, ALU.add))
            then(V.tensor_scalar(tab[:, 1, :], tab[:, 0, :], 0.0, None, ALU.is_lt))
            then(V.tensor_scalar(tab[:, 2, :], tab[:, 0, :], 0.0, None, ALU.is_gt))
            then(V.tensor_tensor(tab[:, 0, :], tab[:, 2, :], tab[:, 1, :], ALU.subtract))
            dve.wait_ge(c_pool, 1)
            then(V.tensor_tensor(tab[:, 2, :], tab[:, 0, :], tab[:, 4, :], ALU.mult))
            then(V.tensor_scalar(tab[:, 1, :], tab[:, 2, :], st[:, 9, 0:1], None, ALU.mult))
            dve.wait_ge(c_pe, 1)
            then(V.tensor_scalar(hidden[:, 0:TABLE], M[0][:, 0:TABLE], cpbb1[:, 0:1], 0.0, ALU.add, ALU.max))
            dve.wait_ge(c_pe, 3)
            then(V.memset(tbs[:], 0.0))
            then(V.tensor_copy(tbs[:, 0, :], M[1][0:TCH, 0:HEADS]))
            then(V.tensor_copy(tbs[0:TABLE - TCH, 1, :], M[1][0:TABLE - TCH, 8:8 + HEADS]))
            dve.wait_ge(c_pe, 4)
            dve.wait_ge(c_zero, ZEROED)
            then(V.tensor_copy(bias_t[:], S[0][0:R, 0:HK]))
            for v in range(4):
                then(V.tensor_copy(bias_hi[0:R, v, :], bias_t[:]))
            V.tensor_tensor(bias_lo[0:R, :], bias_t[:], bias_hi[0:R, 0, :], ALU.subtract).then_inc(c_bias, 1)
            then(V.tensor_scalar(w1s[:], w1[:], n2w[:, 0:1], ZSCALE, ALU.mult, ALU.mult))
            then(V.tensor_copy(w1p[:, 0, :], w1s[:]))
            then(V.tensor_tensor(w1p[:, 1, :], w1s[:], w1p[:, 0, :], ALU.subtract))
            dve.wait_ge(c_pe, 6)
            then(V.tensor_tensor(b1z[:], b1[:], M[2][:, 0:2], ALU.add))
            then(V.tensor_copy(identh[:], ident[:]))
            for n in range(2):
                then(V.tensor_copy(nmT[n][0:R0, 0:R0], ident[0:R0, 0:R0]))
                then(V.tensor_copy(nm[n][:, 0:R - R0], ident[0:R, R0:R]))
            then(V.tensor_scalar(wqkv[:, 0:C], wqkv[:, 0:C], float(D) ** -0.5, None, ALU.mult))
            for b in range(2):
                then(V.memset(vx[b][:], 0.0))
                then(V.memset(vx[b][0:N, :, :, 2 * D:2 * D + 1], 1.0))
                then(V.memset(vx[b][W0:W0 + N, :, :, 2 * D + 1:2 * D + 2], 1.0))
            V.memset(O[:], 1.0).then_inc(c_ready, 1)
            dve.wait_ge(c_ready, 1)

            def statistics(src, stats_b, s_stat):
                for p in range(PAIRS):
                    V.bn_stats(stats_b[:, p, :], src[:, p, :]).then_inc(s_stat, 1)

            def aggregate(stats_b, mv_b, s_stat):
                for p in range(PAIRS):
                    V.bn_aggr(mv_b[:, p, :], stats_b[:, p, :]).then_inc(s_stat, 1)

            def add_eps(mv_b, veps_b, s_stat, s_rs_b, u, scale=1.0):
                dve.wait_ge(s_stat, 9 * u + 8)
                if later(u):
                    dve.wait_ge(s_rs_b, u)
                V.tensor_scalar(veps_b[:], mv_b[:, :, 1], EPS, scale, ALU.add, ALU.mult).then_inc(s_stat, 1)

            def ln1_stats(u, b):
                dve.wait_ge(s_x[b], 32 * u + 32)
                if later(u):
                    dve.wait_ge(s_y0[b], u)
                statistics(xin[b], stats[b], s_st[b])

            def ln1_aggregate(b):
                aggregate(stats[b], mv[b], s_st[b])

            def ln1_eps(u, b):
                add_eps(mv[b], veps[b], s_st[b], s_rs[b], u)

            def ln2_stats_ready(u, b):
                dve.wait_ge(s_x1[b], u + 1)
                if later(u):
                    dve.wait_ge(s_z0[b], u)

            def ln2_stats(u, b):
                statistics(resid(u, b), stats2[b], s_st2[b])

            def ln2_aggregate(u, b):
                aggregate(stats2[b], mv2[b], s_st2[b])
                add_eps(mv2[b], veps2[b], s_st2[b], s_rs2[b], u, ZSCALE ** -2.0)

            def low_parts(u, b):
                for h in range(2):
                    bank = M[h][0:R, 0:2 * 3 * C].rearrange("r (p f) -> r p f", p=2)
                    dve.wait_ge(s_vs[b], 2 * u + h + 1)
                    V.tensor_tensor(qkp[b][:, h::2, :, D:2 * D],
                                    bank[:, :, 0:2 * C].rearrange("r p (h d) -> r p h d", d=D),
                                    qkp[b][:, h::2, :, 0:D], ALU.subtract).then_inc(s_lo[b], 1)

            def repeat_parts(u, b):
                dve.wait_ge(s_lo[b], 2 * u + 2)
                q, k = qkp[b][:, :, 0:HEADS, :], qkp[b][:, :, HEADS:QKH, :]
                V.tensor_copy(q[:, :, :, 2 * D:4 * D], q[:, :, :, 0:2 * D]).then_inc(s_dup[b], 1)
                V.tensor_copy(k[:, :, :, 2 * D:3 * D], k[:, :, :, D:2 * D]).then_inc(s_dup[b], 1)
                V.tensor_copy(k[:, :, :, 3 * D:4 * D], k[:, :, :, 0:D]).then_inc(s_dup[b], 1)

            def place_k(u, b):
                dve.wait_ge(s_kTp[b], u + 1)
                if later(u):
                    dve.wait_ge(s_sc, U * (u - 1) + 4 * b + 4)
                for h in range(2):
                    rows = slice(HR * h, HR * h + HR)
                    V.tensor_copy(kx[b][rows, h], tokens16(M[1], rows)).then_inc(s_kx[b], 1)

            def place_v(u, b, w):
                dve.wait_ge(s_vs[b], 2 * u + 2)
                if later(u):
                    dve.wait_ge(s_pv, U * (u - 1) + 4 * b + 4)
                src = vs[b][:].rearrange("n p (h e d) -> n e p h d", h=4, e=2)
                dst = vx[b][:].rearrange("n (p w) h f -> n w p h f", w=2)
                for e in range(2):
                    V.tensor_copy(dst[W0 * e:W0 * e + N, w, :, :, D * e:D * e + D],
                                  src[W0 * w:W0 * w + N, e]).then_inc(s_vx[b], 1)

            def neg_max(u, j):
                n = U * u + j
                dve.wait_ge(s_sc, n + 1)
                if later(u) or j >= 2:
                    dve.wait_ge(s_nmp, n - 1)
                V.tensor_reduce(nm[j % 2][:, R - R0:R - R0 + HEADS], S[j % 2][0:R, 0:HK].rearrange("q (h n) -> q h n", n=N),
                                AX_X, ALU.max, negate=True).then_inc(s_nm, 1)

            def evac_nmT(u, j):
                n = U * u + j
                dve.wait_ge(s_nmp, n + 1)
                if later(u) or j >= 2:
                    dve.wait_ge(s_sh, n - 1)
                V.tensor_copy(nmT[j % 2][R0:128, 0:R], O[R0:128, NMT_COL:NMT_COL + 57].bitcast(F16)[:, 0:R]).then_inc(s_nmT, 1)

            def evac_o0(u):
                dve.wait_ge(s_oTp[0], u + 1)
                if later(u):
                    dve.wait_ge(s_pj[0], u)
                V.tensor_copy(oT[0][:, :, 0:R], M[0][:, 2 * R:4 * R].rearrange("c (p r) -> c p r", p=2)).then_inc(s_oT[0], 1)

            def evac_y1(u):
                dve.wait_ge(s_yTp[1], u + 1)
                if later(u):
                    dve.wait_ge(s_qkv[1], 2 * u)
                V.tensor_scalar(yT[1][:, :, 0:R], M[0][:, 0:2 * R].rearrange("c (p r) -> c p r", p=2),
                                n1w[:, 0:1], n1b[:, 0:1], ALU.mult, ALU.add).then_inc(s_yT[1], 1)

            def normalise(u, b):
                dve.wait_ge(s_pv, U * u + 4 * b + 4)
                if later(u):
                    dve.wait_ge(s_on[b], u)
                o = O[0:R, 0:PAIRS * 4 * VC].rearrange("r (a f) -> r a f", f=VC)
                V.reciprocal(rec[b][:], o[:, :, 2 * D:VC]).then_inc(s_rec[b], 1)
                dve.wait_ge(s_rec[b], u + 1)
                if later(u):
                    dve.wait_ge(s_oTp[b], u)
                V.tensor_tensor(on[b][:].rearrange("r p (h e d) -> r (p h) e d", e=2, d=D),
                                o[:, :, 0:2 * D].rearrange("r a (e d) -> r a e d", d=D),
                                rec[b][:].unsqueeze(3).broadcast_to([R, 4 * PAIRS, 2, D]), ALU.mult).then_inc(s_on[b], 1)

            def add_attention(u, b):
                dve.wait_ge(s_pj[b], u + 1)
                dve.wait_ge(s_xres[b], u + 1)
                V.tensor_tensor(resid(u, b), M[2][0:R, 0:PAIRS * C].rearrange("r (p c) -> r p c", p=PAIRS), resid(u, b),
                                ALU.add).then_inc(s_x1[b], 1)

            def evac_zT(u, b):
                dve.wait_ge(s_zTp[b], u + 1)
                if later(u):
                    dve.wait_ge(s_f[b], 2 * u)
                V.tensor_copy(zT[b][:].rearrange("c (w n) -> c w n", n=N),
                              M[3][:, 0:4 * W0].bitcast(F16).rearrange("c (w n) -> c w n", n=W0)[:, :, 0:N]).then_inc(s_zT[b], 1)

            def result(u, b):
                dve.wait_ge(s_mo[b], u + 1)
                if later(u):
                    dve.wait_ge(s_out[b], 32 * u)
                V.tensor_tensor(res[b][:], M[3 - b][0:R, 0:PAIRS * C].rearrange("r (p c) -> r p c", p=PAIRS), resid(u, b),
                                ALU.add).then_inc(s_res[b], 1)

            def body(i):
                c, d, a = i - 1, i - 2, i + 1
                for k in range(U):
                    if k == 1 and on_chip(c):
                        dve.wait_ge(s_st2[0], 9 * c + 4)
                    if k == 4 and on_chip(a):
                        dve.wait_ge(s_st[1], 9 * a + 4)
                    if k == 5 and on_chip(c):
                        dve.wait_ge(s_st2[1], 9 * c + 4)
                    u, j = at_unit(i, k, 1)
                    if on_chip(u):
                        evac_nmT(u, j)
                    if k == 5 and on_chip(c):
                        ln2_aggregate(c, 1)
                    if k == 6 and on_chip(a):
                        repeat_parts(a, 0)
                    if k == 7 and on_chip(c):
                        evac_zT(c, 1)
                    if on_chip(i):
                        neg_max(i, k)
                    if k == 0:
                        if on_chip(a):
                            ln1_stats(a, 0)
                            dve.wait_ge(s_st[0], 9 * a + 4)
                        if on_chip(c):
                            add_attention(c, 0)
                        if on_chip(a):
                            ln1_aggregate(0)
                        if on_chip(c):
                            ln2_stats_ready(c, 0)
                        if on_chip(a):
                            ln1_eps(a, 0)
                        if on_chip(c):
                            ln2_stats(c, 0)
                    if k == 1:
                        if on_chip(c):
                            ln2_aggregate(c, 0)
                        if on_chip(i):
                            low_parts(i, 1)
                            repeat_parts(i, 1)
                    if k == 2:
                        if on_chip(c):
                            normalise(c, 1)
                        if on_chip(i):
                            place_k(i, 1)
                    if k == 3:
                        if on_chip(d):
                            result(d, 0)
                            result(d, 1)
                        if on_chip(a):
                            ln1_stats(a, 1)
                    if k == 4:
                        if on_chip(a):
                            ln1_aggregate(1)
                            ln1_eps(a, 1)
                        if on_chip(c):
                            add_attention(c, 1)
                            ln2_stats_ready(c, 1)
                        if on_chip(i):
                            place_v(i, 1, 0)
                        if on_chip(c):
                            ln2_stats(c, 1)
                        if on_chip(i):
                            place_v(i, 1, 1)
                    if k == 5 and on_chip(a):
                        low_parts(a, 0)
                    if k == 6:
                        if on_chip(i):
                            normalise(i, 0)
                        if on_chip(a):
                            place_k(a, 0)
                    if k == 7:
                        if on_chip(i):
                            evac_o0(i)
                        if on_chip(a):
                            evac_y1(a)
                            place_v(a, 0, 0)
                            place_v(a, 0, 1)

            rounds(dve, body)

        @block.tensor
        def _(pe):
            MM = nc.tensor.matmul
            pe.wait_ge(c_in, 16 * N_IN)
            pe.wait_ge(c_chain, C_TAB)
            MM(M[0][:, 0:TABLE], cpbw1[:], tab[:, 1, :], start=True, stop=True).then_inc(c_pe, 1)
            pe.wait_ge(c_chain, C_HID)
            for ch in range(2):
                rows = min(TCH, TABLE - ch * TCH)
                MM(M[1][0:rows, 8 * ch:8 * ch + HEADS], hidden[:, ch * TCH:ch * TCH + rows], cpbw2[:],
                   start=True, stop=True).then_inc(c_pe, 1)
            pe.wait_ge(c_chain, C_TBS)
            for key in range(N):
                for ch in range(2):
                    mm = MM(S[0][0:R, 0:HK].rearrange("q (h n) -> q h n", n=N)[:, :, key], onehot[:, ch, key, :], tbs[:, ch, :],
                            start=(ch == 0), stop=(ch == 1))
            mm.then_inc(c_pe, 1)
            for c in range(2):
                MM(M[2][:, c:c + 1], w1[0:C, 128 * c:128 * c + 128], n2b[0:C, 0:1], start=True, stop=True).then_inc(c_pe, 1)
            pe.wait_ge(c_ready, 1)
            pe.wait_ge(c_zero, ZEROED)
            pe.wait_ge(c_spread, 16 * 9)

            def bias_and_mask(u, j):
                b, p = j // 4, j % 4
                row = ((u % 4) // 3) if b == 1 else 0
                if isinstance(row, int):
                    return bias_hi[:, 2 * row + (p == 3), :]
                return bias_hi[:, bass.ds(row * 2 + (p == 3), 1), :].rearrange("q o f -> q (o f)")

            def scores(u, j):
                n, b, p = U * u + j, j // 4, j % 4
                if later(u) or j >= 2:
                    pe.wait_ge(s_e, n - 1)
                if p == 0:
                    pe.wait_ge(s_qx[b], u + 1)
                    pe.wait_ge(s_kx[b], 2 * (u + 1))
                    pe.wait_ge(s_kx3[b], 2 * (u + 1))
                bank = S[j % 2]
                MM(bank[0:R, 0:HK], left[:, 0:R], bias_and_mask(u, j), start=True, stop=False, skip_group_check=True)
                for w in range(2):
                    for g in range(2):
                        mm = MM(bank[W0 * w:W0 * w + N, 4 * N * g:4 * N * (g + 1)], qx[b][:, 4 * g + p, w, :],
                                kx[b][:, :, 4 * g + p, w, :], start=False, stop=False, skip_group_check=True)
                mm.then_inc(s_sc, 1)

            def turn_max(u, j):
                n = U * u + j
                pe.wait_ge(s_nm, n + 1)
                if j == 6:
                    pe.wait_ge(s_on[0], u + 1)
                elif j == 2 and later(u):
                    pe.wait_ge(s_on[1], u)
                nc.tensor.transpose(O[R0:128, NMT_COL:NMT_COL + 57].bitcast(F16)[:, 0:R], nm[j % 2][:],
                                    identh[0:R, 0:R], tile_position=(0, R0)).then_inc(s_nmp, 1)

            def shift(u, j):
                n = U * u + j
                pe.wait_ge(s_nmT, n + 1)
                MM(S[j % 2][0:R, 0:HK], nmT[j % 2][:, 0:R], bias_lo[:], start=False, stop=True,
                   skip_group_check=True).then_inc(s_sh, 1)

            def turn_probs(u, j):
                n = U * u + j
                pe.wait_ge(s_e, n + 1)
                if later(u) or j >= 1:
                    pe.wait_ge(s_pT, n)
                src = probs[j % 2][:].rearrange("q h n -> q (h n)")
                for hp in range(4):
                    mm = nc.tensor.transpose(PT[0:R, R * hp:R * hp + R], src[:, 2 * W0 * hp:2 * W0 * hp + R],
                                             ident[0:R, 0:R])
                mm.then_inc(s_pTp, 1)

            def times_v(u, j):
                n, b, p = U * u + j, j // 4, j % 4
                pe.wait_ge(s_pT, n + 1)
                if p == 0:
                    pe.wait_ge(s_vx[b], 4 * u + 4)
                    if b == 1:
                        pe.wait_ge(s_on[0], u + 1)
                    elif later(u):
                        pe.wait_ge(s_on[1], u)
                for hp in range(4):
                    for w in range(2):
                        mm = MM(O[W0 * w:W0 * w + N, (4 * p + hp) * VC:(4 * p + hp + 1) * VC],
                                pT[j % 2][:, hp, W0 * w:W0 * w + N], vx[b][:, 2 * p + w, hp, :],
                                start=True, stop=True, tile_position=(0, W0 * w))
                mm.then_inc(s_pv, 1)

            def turn_tokens(dst, src, cols, sem_out):
                tokens = src[:].rearrange("r p c -> r (p c)")
                for pp in range(2):
                    mm = nc.tensor.transpose(dst[:, cols * pp:cols * pp + R], tokens[:, 2 * C * pp:2 * C * pp + 2 * C],
                                             ident[0:R, 0:R])
                mm.then_inc(sem_out, 1)

            def turn_y(u, b):
                pe.wait_ge(s_y1[b], u + 1)
                turn_tokens(M[0][:, 0:2 * R], y1[b], R, s_yTp[b])

            def turn_o(u, b):
                pe.wait_ge(s_on[b], u + 1)
                turn_tokens(M[0][:, 2 * R:4 * R], on[b], R, s_oTp[b])

            def turn_z(u, b):
                pe.wait_ge(s_zp[b], 2 * u + 2)
                dst = M[3][:, 0:4 * W0].bitcast(F16).rearrange("c (p r) -> c p r", p=PAIRS)
                src = zp[b][:].rearrange("r p s c -> r p (s c)")
                for p in range(PAIRS):
                    mm = nc.tensor.transpose(dst[:, p, 0:R], src[:, p, :], identh[0:R, 0:R])
                mm.then_inc(s_zTp[b], 1)

            def project_qkv(u, b):
                pe.wait_ge(s_yT[b], u + 1)
                for pp in range(2):
                    for h in range(2):
                        rows = slice(C * h, C * h + C)
                        mm = MM(M[h][0:R, 3 * C * pp:3 * C * (pp + 1)], yT[b][rows, pp, 0:R], wqkv[rows, :],
                                start=True, stop=True)
                        if pp == 1:
                            mm.then_inc(s_qkv[b], 1)

            def turn_qk(u, b, m):
                pe.wait_ge(s_dup[b], 3 * u + 3)
                dst = M[m][:].bitcast(F16).rearrange("c (a n) -> c a n", n=2 * W0)
                src = qkp[b][:].rearrange("r p h f -> r p (h f)")
                for g in range(2):
                    for p in range(PAIRS):
                        first = (2 * m + g) * 4 * HR
                        mm = nc.tensor.transpose(dst[:, 4 * g + p, 0:R], src[:, p, first:first + 4 * HR], identh[0:R, 0:R])
                mm.then_inc((s_qTp, s_kTp)[m][b], 1)

            def project_out(u, b):
                pe.wait_ge(s_oT[b], u + 1)
                for pp in range(2):
                    mm = MM(M[2][0:R, 2 * C * pp:2 * C * (pp + 1)], oT[b][:, pp, 0:R], wproj[:], start=True, stop=True)
                mm.then_inc(s_pj[b], 1)

            def fc1(u, b, m0_free=()):
                pe.wait_ge(s_zT[b], u + 1)
                for c in FC_ORDER[b]:
                    if b == 1 and c == 0:
                        after(*m0_free)
                    for part in range(2):
                        mm = MM(M[FC_BANK[b] + c][:, 0:T], w1p[:, part, 128 * c:128 * c + 128], zT[b][:],
                                start=(part == 0), stop=(part == 1))
                    mm.then_inc(s_f[b], 1)

            def fc2(u, b):
                pe.wait_ge(s_g[b], 2 * u + 2)
                tokens = gl[b][:].rearrange("f c (p h t) -> f c p h t", p=2, h=2)
                for h in range(2):
                    for c in range(2):
                        mm = MM(M[3 - b][C * h:C * h + C, 0:T // 2], w2[:, c, :], tokens[:, c, :, h, :],
                                start=(c == 0), stop=(c == 1), tile_position=(0, C * h))
                mm.then_inc(s_m[b], 1)

            def turn_back(u, b):
                pe.wait_ge(s_mT[b], u + 1)
                src = mT[b][:].rearrange("c w n -> c (w n)")
                for pp in range(2):
                    mm = nc.tensor.transpose(M[3 - b][0:R, 2 * C * pp:2 * C * pp + 2 * C], src[:, 2 * W0 * pp:2 * W0 * pp + R],
                                             ident[:])
                mm.then_inc(s_mo[b], 1)

            def after(*uses):
                for u, semaphore, count in uses:
                    if on_chip(u):
                        pe.wait_ge(semaphore, count)
                        return

            def body(i):
                c, d = i - 1, i - 2
                a = i + 1
                y = [(a, s_yT[b], a + 1) for b in range(2)]
                o_c1, o_i0 = (c, s_oT[1], c + 1), (i, s_oT[0], i + 1)
                proj = [(c, s_x1[b], c + 1) for b in range(2)]
                z = [(c, s_zT[b], c + 1) for b in range(2)]
                q_i1, k_i1 = (i, s_qx[1], i + 1), (i, s_kx[1], 2 * i + 2)
                q_a0, k_a0 = (a, s_qx[0], a + 1), (a, s_kx[0], 2 * a + 2)
                back = [(d, s_res[b], d + 1) for b in range(2)]
                k3_i1, k3_a0 = (i, s_kx3[1], 2 * i + 2), (a, s_kx3[0], 2 * a + 2)
                gelu_d1 = (d, s_g[1], 2 * d + 2)
                gelu_d0 = (d, s_g[0], 2 * d + 2)
                for k in range(U):
                    u1, j1 = at_unit(i, k, 1)
                    if on_chip(u1):
                        turn_max(u1, j1)
                    if on_chip(i):
                        scores(i, k)
                    u2, j2 = at_unit(i, k, 2)
                    if on_chip(u2):
                        turn_probs(u2, j2)
                    if k == 7 and on_chip(c):
                        after(z[0])
                        turn_z(c, 1)
                    if on_chip(u1):
                        shift(u1, j1)
                    u3, j3 = at_unit(i, k, 3)
                    if on_chip(u3):
                        times_v(u3, j3)
                    if k == 5 and on_chip(c):
                        turn_z(c, 0)
                    if k == 0:
                        if on_chip(c):
                            after(gelu_d0)
                            project_out(c, 0)
                        if on_chip(d):
                            fc2(d, 0)
                        if on_chip(i):
                            after(gelu_d1)
                            project_qkv(i, 1)
                    if k == 1:
                        if on_chip(d):
                            after(proj[0])
                            fc2(d, 1)
                    if k == 2:
                        if on_chip(i):
                            turn_qk(i, 1, 0)
                            turn_qk(i, 1, 1)
                        if on_chip(d):
                            turn_back(d, 0)
                        if on_chip(d):
                            turn_back(d, 1)
                    if k == 3:
                        after(q_i1, gelu_d1)
                        if on_chip(a):
                            turn_y(a, 0)
                        if on_chip(c):
                            turn_o(c, 1)
                    if k == 4:
                        if on_chip(c):
                            after(back[1], proj[0])
                            project_out(c, 1)
                        if on_chip(a):
                            after(o_c1)
                            after(k_i1)
                            after(k3_i1)
                            project_qkv(a, 0)
                    if k == 6:
                        if on_chip(a):
                            turn_qk(a, 0, 0)
                            turn_qk(a, 0, 1)
                    if k == 7:
                        after(q_a0, o_c1)
                        if on_chip(a):
                            turn_y(a, 1)
                        if on_chip(i):
                            turn_o(i, 0)
                        if on_chip(c):
                            after(proj[1])
                            pe.wait_ge(s_zT[1], c + 1)
                            fc1(c, 0)
                            after(k_a0, k_i1)
                            after(k3_a0, k3_i1)
                            fc1(c, 1, (y[1], o_i0, o_c1))

            rounds(pe, body)


def shape_constants():
    ident = np.eye(128, dtype=np.float32)
    co = np.stack(np.meshgrid(np.arange(WIN), np.arange(WIN), indexing="ij")).reshape(2, -1)
    rel = co[:, :, None] - co[:, None, :]
    idx = (rel[0] + WIN - 1) * (2 * WIN - 1) + rel[1] + WIN - 1
    onehot = np.zeros((2 * TCH, N, R), np.float32)
    for q in range(N):
        for k in range(N):
            for w in range(2):
                onehot[idx[q, k], k, W0 * w + q] = 1.0
    onehot = np.ascontiguousarray(onehot.reshape(2, TCH, N, R))
    left = np.zeros((128, TP), np.float16)
    left[:R, :R] = np.eye(R)
    left[N:W0] = 0
    right = np.zeros((4, 2, 8, HEADS, N), np.float16)
    part = np.where(np.arange(WIN) < WIN - SHIFT, 0, 1)
    prow, pcol = part[co[0]], part[co[1]]
    for w in range(2):
        for r in range(2):
            for c in range(2):
                row = 4 * w + 2 * r + c
                for first in (N, R):
                    left[first + row, W0 * w:W0 * w + N] = np.where((prow == r) & (pcol == c), -40000.0, 0.0)
                for v in range(4):
                    unseen = ((prow != r) & bool(v // 2)) | ((pcol != c) & bool(v % 2 and w == 1))
                    for n, factor in enumerate((24992.0, 8.0)):
                        right[v, n, row] = np.where(unseen, factor, 0.0)
    line = (np.arange(-(WIN - 1), WIN, dtype=np.float32) / np.float32(WIN - 1)).astype(np.float32)
    grid = np.stack(np.meshgrid(line, line, indexing="ij")).reshape(2, -1).astype(np.float32)
    headsel = np.zeros((HEADS, HEADS, N), np.float16)
    for h in range(HEADS):
        headsel[h, h] = 1.0
    return ident, onehot, left, right.reshape(4, 2, 8, HK), np.ascontiguousarray(grid), headsel.reshape(HEADS, HK)


def kernel(x, L0_conv_norm1_w, L0_conv_norm1_b, L0_conv_qkv_w, L0_conv_proj_w, L0_conv_proj_b, L0_conv_cpb_w1,
           L0_conv_cpb_b1, L0_conv_cpb_w2, L0_conv_h_times, L0_conv_pow_para, L0_conv_ws_scalar, L0_conv_ws_scalar2,
           L0_conv_norm2_w, L0_conv_norm2_b, L0_conv_fc1_w, L0_conv_fc1_b, L0_conv_fc2_w, L0_conv_fc2_b):
    import concourse.bacc as bacc
    from concourse.bass_utils import run_bass_kernel_spmd

    B, H, W, _ = x.shape
    nh, nw = H // WIN, W // WIN

    def rows(a):
        return np.broadcast_to(np.asarray(a).reshape(1, -1), (R, np.asarray(a).size))

    xs = np.roll(np.asarray(x), (-SHIFT, -SHIFT), axis=(1, 2))
    xs = xs.reshape(B, nh, WIN, PAIRS, 2, WIN, C).transpose(0, 1, 4, 2, 5, 3, 6).reshape(B * nh, 2, N, PAIRS, C)
    ident, onehot, left, right, grid, headsel = shape_constants()
    twice = lambda a: np.tile(np.asarray(a).reshape(C, 1), (2, 1))
    two = lambda a: np.broadcast_to(np.asarray(a).reshape(1, 1), (2, 1))
    fc2_wT = np.asarray(L0_conv_fc2_w).T.reshape(2, 128, C).transpose(1, 0, 2)
    ins = {
        "x": xs, "norm1_w": twice(L0_conv_norm1_w), "norm1_b": twice(L0_conv_norm1_b),
        "qkv_wT": np.asarray(L0_conv_qkv_w).T, "proj_wT": np.asarray(L0_conv_proj_w).T, "proj_b": rows(L0_conv_proj_b),
        "cpb_w1T": np.asarray(L0_conv_cpb_w1).T, "cpb_b1": np.asarray(L0_conv_cpb_b1).reshape(-1, 1),
        "cpb_w2T": np.asarray(L0_conv_cpb_w2).T, "h_times": two(L0_conv_h_times), "pow_para": two(L0_conv_pow_para),
        "ws_scalar": two(L0_conv_ws_scalar), "ws_scalar2": two(L0_conv_ws_scalar2),
        "norm2_w": twice(L0_conv_norm2_w), "norm2_b": twice(L0_conv_norm2_b), "fc1_wT": np.asarray(L0_conv_fc1_w).T,
        "fc1_b": np.asarray(L0_conv_fc1_b).reshape(2, 128).T, "fc2_wT": fc2_wT, "fc2_b": twice(L0_conv_fc2_b),
        "c_ident": ident, "c_onehot": onehot, "c_left": left, "c_right": right, "c_grid": grid, "c_headsel": headsel,
    }
    nc = bacc.Bacc("TRN2", target_bir_lowering=False, num_devices=1)
    arrays, aps = {}, {}
    for name, a in ins.items():
        a = np.ascontiguousarray(a)
        arrays["in_" + name] = a
        aps[name] = nc.dram_tensor("in_" + name, a.shape, mybir.dt.from_np(a.dtype), kind="ExternalInput").ap()
    out = nc.dram_tensor("out", xs.shape, F32, kind="ExternalOutput").ap()
    swin_block(nc, out=out, **aps)
    r = run_bass_kernel_spmd(nc, [arrays], core_ids=[0])
    got = r.results[0]["out"]
    got = got.reshape(B, nh, 2, WIN, WIN, PAIRS, C).transpose(0, 1, 3, 5, 2, 4, 6).reshape(B, H, W, C)
    return np.roll(got, (SHIFT, SHIFT), axis=(1, 2))
```
